# Optimizing a Trainium2 kernel written in Bass

```python
import numpy as np
import jax
import jax.numpy as jnp

def _softmax(x, axis=-1):
    return jax.nn.softmax(x, axis=axis)

def _gelu(x):
    return jax.nn.gelu(x, approximate=True)

def _silu(x):
    return jax.nn.silu(x)

def _sigmoid(x):
    return jax.nn.sigmoid(x)

def _layernorm(x, axis=-1, eps=1e-05):
    m = jnp.mean(x, axis=axis, keepdims=True)
    v = jnp.var(x, axis=axis, keepdims=True)
    return (x - m) / jnp.sqrt(v + eps)

def _scatter_add(tgt, idx, src, axis=0):
    return tgt.at[idx].add(src)

def _segment_sum(src, seg, n):
    return jax.ops.segment_sum(src, seg, n)
kernel_name = 'mk_vit_tower_cls_d2_tok_img1024_r4_f848ba'

def setup_inputs(seed: int=0):
    np.random.seed(seed)
    _w = jnp.asarray

    def _rec_inputs():
        import jax
        import jax.numpy as jnp
        _rk = jax.random.key(seed)
        x = -0.00016672 + 0.999947 * jax.random.normal(jax.random.fold_in(_rk, 1), (16, 3, 96, 96), jnp.float32)
        cls_tok = 0.02 * jax.random.normal(jax.random.fold_in(_rk, 5), (1, 1, 256), jnp.float32)
        return (x, cls_tok)
    x, cls_tok = _rec_inputs()

    def _L0_tok_setup():
        import jax, jax.numpy as jnp
        import numpy as np
        IMG = 96
        PATCH = 16
        C_IN = 3
        EMBED = 256
        NPH = IMG // PATCH
        NUM_PATCHES = NPH * NPH
        PATCH_DIM = PATCH * PATCH * C_IN
        key = jax.random.key(seed)
        k_x, k_w, k_b, k_cls, k_pos = jax.random.split(key, 5)
        x = jax.random.normal(k_x, (64, C_IN, IMG, IMG), dtype=jnp.float32)
        W = jax.random.normal(k_w, (EMBED, PATCH_DIM), dtype=jnp.float32) * (1.0 / np.sqrt(PATCH_DIM))
        b = jax.random.normal(k_b, (EMBED,), dtype=jnp.float32) * 0.01
        cls_token = jax.random.normal(k_cls, (1, 1, EMBED), dtype=jnp.float32) * 0.02
        pos_embed = jax.random.normal(k_pos, (1, NUM_PATCHES + 1, EMBED), dtype=jnp.float32) * 0.02
        return {'x': x, 'W': W, 'b': b, 'cls_token': cls_token, 'pos_embed': pos_embed}
    _L0_tok_all = _L0_tok_setup()
    _L0_tok_in = {k: v for k, v in _L0_tok_all.items() if k in ('W', 'b', 'cls_token', 'pos_embed')}
    del _L0_tok_all

    def _L0_attn_setup():
        import jax, jax.numpy as jnp
        import numpy as np
        import math
        EMBED_DIM = 256
        NUM_HEADS = 8
        DEPTH = 12
        HEAD_DIM = EMBED_DIM // NUM_HEADS // 2
        LAMBDA_INIT = 0.8 - 0.6 * math.exp(-0.3 * DEPTH)
        EPS = 1e-08

        def _rotary(t):
            d = t.shape[-1]
            s = t.shape[1]
            inv_freq = 1.0 / 10000.0 ** (jnp.arange(0, d, 2, dtype=jnp.float32) / d)
            pos = jnp.arange(s, dtype=jnp.float32)
            freqs = pos[:, None] * inv_freq[None, :]
            freqs = jnp.repeat(freqs, 2, axis=-1)
            cos = jnp.cos(freqs)[None, :, None, :]
            sin = jnp.sin(freqs)[None, :, None, :]
            x = t.reshape(t.shape[:-1] + (d // 2, 2))
            x1, x2 = (x[..., 0], x[..., 1])
            rot = jnp.stack([-x2, x1], axis=-1).reshape(t.shape)
            return t * cos + rot * sin

        def _sdpa_over_heads(q, k, v):
            scores = jnp.einsum('bsnd,bsmd->bsnm', q, k) / HEAD_DIM ** 0.25
            aw = jax.nn.softmax(scores, axis=-1)
            return jnp.einsum('bsnm,bsme->bsne', aw, v)
        key = jax.random.key(seed)
        ks = jax.random.split(key, 10)
        E, H, D = (EMBED_DIM, NUM_HEADS, HEAD_DIM)
        scale = 1.0 / np.sqrt(E)
        return {'x': jax.random.normal(ks[0], (4, 1024, E), jnp.float32), 'Wq': jax.random.normal(ks[1], (E, E), jnp.float32) * scale, 'Wk': jax.random.normal(ks[2], (E, E), jnp.float32) * scale, 'Wv': jax.random.normal(ks[3], (E, E), jnp.float32) * scale, 'Wo': jax.random.normal(ks[4], (E, E), jnp.float32) * scale, 'lambda_q1': jax.random.normal(ks[5], (D,), jnp.float32) * 0.1, 'lambda_k1': jax.random.normal(ks[6], (D,), jnp.float32) * 0.1, 'lambda_q2': jax.random.normal(ks[7], (D,), jnp.float32) * 0.1, 'lambda_k2': jax.random.normal(ks[8], (D,), jnp.float32) * 0.1, 'ln_w': 1.0 + 0.1 * jax.random.normal(ks[9], (2 * D,), jnp.float32), 'ln_b': jnp.zeros((2 * D,), jnp.float32)}
    _L0_attn_all = _L0_attn_setup()
    _L0_attn_in = {k: v for k, v in _L0_attn_all.items() if k in ('Wq', 'Wk', 'Wv', 'Wo', 'lambda_q1', 'lambda_k1', 'lambda_q2', 'lambda_k2', 'ln_w', 'ln_b')}
    del _L0_attn_all

    def _L0_ffn_setup():
        import jax, jax.numpy as jnp
        import numpy as np
        R = 64
        key = jax.random.key(seed)
        k1, k2, k3 = jax.random.split(key, 3)
        B, S, D_IN, D_OUT = (8, 1024, 256, 256)
        x = jax.random.normal(k1, (B, S, D_IN), dtype=jnp.float32)
        weight = jax.random.normal(k2, (D_OUT, D_IN), dtype=jnp.float32) * (1.0 / np.sqrt(D_IN))
        disha = jax.random.normal(k3, (R, D_OUT), dtype=jnp.float32) * 0.01
        return {'x': x, 'weight': weight, 'disha': disha}
    _L0_ffn_all = _L0_ffn_setup()
    _L0_ffn_in = {k: v for k, v in _L0_ffn_all.items() if k in ('weight', 'disha')}
    del _L0_ffn_all

    def _L1_attn_setup():
        import jax, jax.numpy as jnp
        import numpy as np
        D_MODEL = 256
        NUM_HEADS = 16
        BATCH = 2
        SEQ = 512

        def _trunc_normal(key, shape, std):
            return jax.random.truncated_normal(key, -3.0, 3.0, shape, dtype=jnp.float32) * std
        key = jax.random.key(seed)
        kx, kq, kk, kv, ko = jax.random.split(key, 5)
        std = (2.0 / (D_MODEL + D_MODEL)) ** 0.5
        return {'X': jax.random.normal(kx, (BATCH, SEQ, D_MODEL), dtype=jnp.float32), 'q_proj': _trunc_normal(kq, (D_MODEL, D_MODEL), std), 'k_proj': _trunc_normal(kk, (D_MODEL, D_MODEL), std), 'v_proj': _trunc_normal(kv, (D_MODEL, D_MODEL), std), 'o_proj': _trunc_normal(ko, (D_MODEL, D_MODEL), std)}
    _L1_attn_all = _L1_attn_setup()
    _L1_attn_in = {k: v for k, v in _L1_attn_all.items() if k in ('q_proj', 'k_proj', 'v_proj', 'o_proj')}
    del _L1_attn_all

    def _L1_ffn_setup():
        import jax, jax.numpy as jnp
        import numpy as np
        H = 256
        I = 1024
        E = 4
        LN_EPS = 1e-12

        def _layer_norm(x, gamma, beta, eps=LN_EPS):
            mu = jnp.mean(x, axis=-1, keepdims=True)
            var = jnp.mean(jnp.square(x - mu), axis=-1, keepdims=True)
            return (x - mu) * jax.lax.rsqrt(var + eps) * gamma + beta
        key = jax.random.key(seed)
        ks = jax.random.split(key, 8)
        B, S = (4, 128)
        scale = 0.02
        return {'hidden_states': jax.random.normal(ks[0], (B, S, H), jnp.float32), 'W_router': jax.random.normal(ks[1], (H, E), jnp.float32) * scale, 'W1': jax.random.normal(ks[2], (E, H, I), jnp.float32) * scale, 'b1': jax.random.normal(ks[3], (E, I), jnp.float32) * scale, 'Wo': jax.random.normal(ks[4], (I, H), jnp.float32) * scale, 'bo': jax.random.normal(ks[5], (H,), jnp.float32) * scale, 'ln_gamma': jnp.ones((H,), jnp.float32), 'ln_beta': jnp.zeros((H,), jnp.float32)}
    _L1_ffn_all = _L1_ffn_setup()
    _L1_ffn_in = {k: v for k, v in _L1_ffn_all.items() if k in ('W_router', 'W1', 'b1', 'Wo', 'bo', 'ln_gamma', 'ln_beta')}
    del _L1_ffn_all
    return {'x': x, 'cls_tok': cls_tok, 'L0_tok_W': _L0_tok_in['W'], 'L0_tok_b': _L0_tok_in['b'], 'L0_tok_cls_token': _L0_tok_in['cls_token'], 'L0_tok_pos_embed': _L0_tok_in['pos_embed'], 'L0_attn_Wq': _L0_attn_in['Wq'], 'L0_attn_Wk': _L0_attn_in['Wk'], 'L0_attn_Wv': _L0_attn_in['Wv'], 'L0_attn_Wo': _L0_attn_in['Wo'], 'L0_attn_lambda_q1': _L0_attn_in['lambda_q1'], 'L0_attn_lambda_k1': _L0_attn_in['lambda_k1'], 'L0_attn_lambda_q2': _L0_attn_in['lambda_q2'], 'L0_attn_lambda_k2': _L0_attn_in['lambda_k2'], 'L0_attn_ln_w': _L0_attn_in['ln_w'], 'L0_attn_ln_b': _L0_attn_in['ln_b'], 'L0_ffn_weight': _L0_ffn_in['weight'], 'L0_ffn_disha': _L0_ffn_in['disha'], 'L1_attn_q_proj': _L1_attn_in['q_proj'], 'L1_attn_k_proj': _L1_attn_in['k_proj'], 'L1_attn_v_proj': _L1_attn_in['v_proj'], 'L1_attn_o_proj': _L1_attn_in['o_proj'], 'L1_ffn_W_router': _L1_ffn_in['W_router'], 'L1_ffn_W1': _L1_ffn_in['W1'], 'L1_ffn_b1': _L1_ffn_in['b1'], 'L1_ffn_Wo': _L1_ffn_in['Wo'], 'L1_ffn_bo': _L1_ffn_in['bo'], 'L1_ffn_ln_gamma': _L1_ffn_in['ln_gamma'], 'L1_ffn_ln_beta': _L1_ffn_in['ln_beta']}

def reference(x, cls_tok, L0_tok_W, L0_tok_b, L0_tok_cls_token, L0_tok_pos_embed, L0_attn_Wq, L0_attn_Wk, L0_attn_Wv, L0_attn_Wo, L0_attn_lambda_q1, L0_attn_lambda_k1, L0_attn_lambda_q2, L0_attn_lambda_k2, L0_attn_ln_w, L0_attn_ln_b, L0_ffn_weight, L0_ffn_disha, L1_attn_q_proj, L1_attn_k_proj, L1_attn_v_proj, L1_attn_o_proj, L1_ffn_W_router, L1_ffn_W1, L1_ffn_b1, L1_ffn_Wo, L1_ffn_bo, L1_ffn_ln_gamma, L1_ffn_ln_beta):
    import jax
    import jax.numpy as jnp

    def _L0_tok_ref(x, W, b, cls_token, pos_embed):
        import jax, jax.numpy as jnp
        import numpy as np
        IMG = 96
        PATCH = 16
        C_IN = 3
        EMBED = 256
        NPH = IMG // PATCH
        NUM_PATCHES = NPH * NPH
        PATCH_DIM = PATCH * PATCH * C_IN
        B, C, H, Wd = x.shape
        nph, npw = (H // PATCH, Wd // PATCH)
        patches = x.reshape(B, C, nph, PATCH, npw, PATCH)
        patches = patches.transpose(0, 2, 4, 1, 3, 5)
        patches = patches.reshape(B, nph * npw, C * PATCH * PATCH)
        proj = jnp.einsum('bnd,ed->bne', patches, W) + b
        cls = jnp.broadcast_to(cls_token, (B, 1, cls_token.shape[-1]))
        out = jnp.concatenate([cls, proj], axis=1) + pos_embed
        return out

    def _L0_attn_ref(x, Wq, Wk, Wv, Wo, lambda_q1, lambda_k1, lambda_q2, lambda_k2, ln_w, ln_b):
        import jax, jax.numpy as jnp
        import numpy as np
        import math
        EMBED_DIM = 256
        NUM_HEADS = 8
        DEPTH = 12
        HEAD_DIM = EMBED_DIM // NUM_HEADS // 2
        LAMBDA_INIT = 0.8 - 0.6 * math.exp(-0.3 * DEPTH)
        EPS = 1e-08

        def _rotary(t):
            d = t.shape[-1]
            s = t.shape[1]
            inv_freq = 1.0 / 10000.0 ** (jnp.arange(0, d, 2, dtype=jnp.float32) / d)
            pos = jnp.arange(s, dtype=jnp.float32)
            freqs = pos[:, None] * inv_freq[None, :]
            freqs = jnp.repeat(freqs, 2, axis=-1)
            cos = jnp.cos(freqs)[None, :, None, :]
            sin = jnp.sin(freqs)[None, :, None, :]
            x = t.reshape(t.shape[:-1] + (d // 2, 2))
            x1, x2 = (x[..., 0], x[..., 1])
            rot = jnp.stack([-x2, x1], axis=-1).reshape(t.shape)
            return t * cos + rot * sin

        def _sdpa_over_heads(q, k, v):
            scores = jnp.einsum('bsnd,bsmd->bsnm', q, k) / HEAD_DIM ** 0.25
            aw = jax.nn.softmax(scores, axis=-1)
            return jnp.einsum('bsnm,bsme->bsne', aw, v)
        b, s, E = x.shape
        H, D = (NUM_HEADS, HEAD_DIM)
        q = (x @ Wq).reshape(b, s, 2 * H, D)
        k = (x @ Wk).reshape(b, s, 2 * H, D)
        v = (x @ Wv).reshape(b, s, H, 2 * D)
        q = _rotary(q)
        k = _rotary(k)
        q = q.reshape(b, s, H, 2, D)
        k = k.reshape(b, s, H, 2, D)
        q1, q2 = (q[:, :, :, 0], q[:, :, :, 1])
        k1, k2 = (k[:, :, :, 0], k[:, :, :, 1])
        attn1 = _sdpa_over_heads(q1, k1, v)
        attn2 = _sdpa_over_heads(q2, k2, v)
        lam = jnp.exp(jnp.sum(lambda_q1 * lambda_k1)) - jnp.exp(jnp.sum(lambda_q2 * lambda_k2)) + LAMBDA_INIT
        a = attn1 - lam * attn2
        rms = jax.lax.rsqrt(jnp.mean(a * a, axis=-1, keepdims=True) + EPS)
        a = a * rms * ln_w + ln_b
        a = a * (1.0 - LAMBDA_INIT)
        return a.reshape(b, s, E) @ Wo

    def _L0_ffn_ref(x, weight, disha):
        import jax, jax.numpy as jnp
        import numpy as np
        R = 64
        result = jnp.einsum('bsd,od->bso', x, weight)
        r = disha.shape[0]
        pooled = x.reshape(*x.shape[:-1], x.shape[-1] // r, r).sum(axis=-2)
        return result + pooled @ disha

    def _L1_attn_ref(X, q_proj, k_proj, v_proj, o_proj):
        import jax, jax.numpy as jnp
        import numpy as np
        D_MODEL = 256
        NUM_HEADS = 16
        BATCH = 2
        SEQ = 512

        def _trunc_normal(key, shape, std):
            return jax.random.truncated_normal(key, -3.0, 3.0, shape, dtype=jnp.float32) * std
        B, S, D = X.shape
        H = NUM_HEADS
        d_k = D // H
        q_w = q_proj.reshape(H, d_k, D)
        k_w = k_proj.reshape(H, d_k, D)
        v_w = v_proj.reshape(H, d_k, D)
        o_w = o_proj.reshape(D, H, d_k).transpose(1, 0, 2)
        q = jnp.einsum('hkd,bsd->bhsk', q_w, X)
        k = jnp.einsum('hkd,bsd->bhsk', k_w, X)
        v = jnp.einsum('hkd,bsd->bhsk', v_w, X)
        scale = 1.0 / jnp.sqrt(jnp.asarray(d_k, dtype=X.dtype))
        scores = jnp.einsum('bhqk,bhsk->bhqs', q, k) * scale
        causal = jnp.tril(jnp.ones((S, S), dtype=bool))
        scores = jnp.where(causal, scores, jnp.asarray(-jnp.inf, dtype=scores.dtype))
        attn = jax.nn.softmax(scores, axis=-1)
        attn_out = jnp.einsum('bhqs,bhsk->bhqk', attn, v)
        return jnp.einsum('hdv,bhsv->bsd', o_w, attn_out)

    def _L1_ffn_ref(hidden_states, W_router, W1, b1, Wo, bo, ln_gamma, ln_beta):
        import jax, jax.numpy as jnp
        import numpy as np
        H = 256
        I = 1024
        E = 4
        LN_EPS = 1e-12

        def _layer_norm(x, gamma, beta, eps=LN_EPS):
            mu = jnp.mean(x, axis=-1, keepdims=True)
            var = jnp.mean(jnp.square(x - mu), axis=-1, keepdims=True)
            return (x - mu) * jax.lax.rsqrt(var + eps) * gamma + beta
        B, S, _ = hidden_states.shape
        x = hidden_states.reshape(-1, H)
        logits = x @ W_router
        expert_idx = jnp.argmax(logits, axis=-1)
        h = jnp.einsum('th,ehi->tei', x, W1) + b1
        h = jax.nn.gelu(h, approximate=False)
        onehot = jax.nn.one_hot(expert_idx, E, dtype=x.dtype)
        intermediate = jnp.einsum('te,tei->ti', onehot, h)
        y = intermediate @ Wo + bo + x
        y = _layer_norm(y, ln_gamma, ln_beta)
        return y.reshape(B, S, H)
    h = _L0_tok_ref(x, L0_tok_W, L0_tok_b, L0_tok_cls_token, L0_tok_pos_embed)
    h = jnp.concatenate([jnp.broadcast_to(cls_tok, (h.shape[0], 1, h.shape[2])), h], axis=1)
    h = h + _L0_attn_ref(_layernorm(h, axis=-1), L0_attn_Wq, L0_attn_Wk, L0_attn_Wv, L0_attn_Wo, L0_attn_lambda_q1, L0_attn_lambda_k1, L0_attn_lambda_q2, L0_attn_lambda_k2, L0_attn_ln_w, L0_attn_ln_b)
    h = h + _L0_ffn_ref(_layernorm(h, axis=-1), L0_ffn_weight, L0_ffn_disha)
    h = h + _L1_attn_ref(_layernorm(h, axis=-1), L1_attn_q_proj, L1_attn_k_proj, L1_attn_v_proj, L1_attn_o_proj)
    h = h + _L1_ffn_ref(_layernorm(h, axis=-1), L1_ffn_W_router, L1_ffn_W1, L1_ffn_b1, L1_ffn_Wo, L1_ffn_bo, L1_ffn_ln_gamma, L1_ffn_ln_beta)
    return h

_drawn_inputs = setup_inputs


def setup_inputs(seed=0):
    import zlib

    import numpy as np

    out = dict(_drawn_inputs(seed))
    spreads = {'L0_attn_ln_b': (0.0, 0.1), 'L1_ffn_ln_gamma': (1.0, 0.2), 'L1_ffn_ln_beta': (0.0, 0.1)}
    factors = {'L0_tok_b': 4.223,
     'L0_attn_lambda_q1': 8.0,
     'L0_attn_lambda_q2': 8.0,
     'L0_attn_lambda_k2': 5.51,
     'L1_ffn_b1': 8.0,
     'L1_ffn_bo': 6.605}
    for name, (base, spread) in spreads.items():
        noise = np.random.default_rng([zlib.crc32(name.encode()), seed]).standard_normal(out[name].shape)
        drawn = base * np.exp(spread * noise) if base else spread * noise
        out[name] = jnp.asarray(drawn.astype(out[name].dtype))
    for name, factor in factors.items():
        out[name] = (out[name] * factor).astype(out[name].dtype)
    return out
```

```python
from contextlib import ExitStack
import math

import numpy as np
import concourse.bass as bass
from concourse import mybir

F32 = mybir.dt.float32
BF16 = mybir.dt.bfloat16
ALU = mybir.AluOpType
ACT = mybir.ActivationFunctionType
AX = mybir.AxisListType.X

P = 128
B, CIN, IMG, PATCH = 16, 3, 96, 16
NP = IMG // PATCH
PD = CIN * PATCH * PATCH
S = NP * NP + 2
E = 256
EC = E // P
PC = PD // P
G = 2
GB = B // G
TT = 102
GT = 3
GN = GT * TT
NT = G * GT
N = G * GN
H0, D0 = 8, 16
H1, D1 = 16, 16
HC = H1 // EC
KT = 3
KC = -(-H1 // KT)
KR = KT * S
VW = D1 + 1
NX = 4
FF = 1024
FC = FF // P
PAIRS = B // 2
HALF = 64
LAMBDA_INIT = 0.8 - 0.6 * math.exp(-0.3 * 12)
RMS_EPS, LN_EPS, LN_EPS_OUT = 1e-8, 1e-5, 1e-12
SCALE0 = 1.0 / D0 ** 0.25
SCALE1 = 1.0 / D1 ** 0.5
MASKED = -1e30
ROWS = 3 + NP * NP + 1


def tower_kernel(nc, patches, tok_w, rows, sel, wqkv, rope, lam, lnwb, wo0, wf, disha, wq1, wk1, wv1,
                 wo1, hmask, vmask, vones, causal, rowsel, ident_in, wr, w1, b1, wo2, tail, out):
    with ExitStack() as ctx:
        def sb(name, shape, dt=F32):
            return ctx.enter_context(nc.sbuf_tensor(name, shape, dt))

        def sem(name):
            return ctx.enter_context(nc.semaphore(name))

        bank = [ctx.enter_context(nc.psum_tensor(f"bank{i}", [P, 512], F32)) for i in range(8)]

        tok_w_sb = sb("tok_w_sb", [P, PC, E])
        rows_sb = sb("rows_sb", [ROWS, E])
        sel_sb = sb("sel_sb", [ROWS, N])
        wqkv_sb = sb("wqkv_sb", [P, EC, 3 * E])
        rope_sb = sb("rope_sb", [P, NT, 2, D0])
        lam_sb = sb("lam_sb", [P, 2, 2, D0])
        lnwb_sb = sb("lnwb_sb", [P, 2])
        wo0_sb = sb("wo0_sb", [P, EC, E])
        wf_sb = sb("wf_sb", [P, EC, E])
        disha_sb = sb("disha_sb", [P, E])
        wq1_sb = sb("wq1_sb", [P, EC, E])
        wk1_sb = sb("wk1_sb", [P, EC, E])
        wv1_sb = sb("wv1_sb", [P, EC, E])
        wo1_sb = sb("wo1_sb", [P, EC, E])
        hmask_sb = sb("hmask_sb", [P, HC])
        vmask_sb = sb("vmask_sb", [KR, KT, D1])
        causal_f = sb("causal_f", [S, S])
        rowsel_f = sb("rowsel_f", [S, P])
        causal_sb = sb("causal_sb", [S, S], BF16)
        rowsel_sb = sb("rowsel_sb", [S, P], BF16)
        ident = sb("ident", [P, P])
        identb = sb("identb", [P, P], BF16)
        wr_sb = sb("wr_sb", [P, EC, NX])
        w1_sb = sb("w1_sb", [P, EC, NX, FF])
        b1_sb = sb("b1_sb", [NX, FF])
        wo2_sb = sb("wo2_sb", [P, FC, E])
        tail_sb = sb("tail_sb", [P, 3 * E + NX])
        bo_sb = tail_sb[:, 0:E]
        gamma_sb = tail_sb[:, E:2 * E]
        beta_sb = tail_sb[:, 2 * E:3 * E]
        tie_sb = tail_sb[:, 3 * E:3 * E + NX]
        expo = sb("expo", [P, 16])

        h = sb("h", [P, NT, E])
        xn = sb("xn", [P, NT, E])
        xT = sb("xT", [P, EC, TT])
        x1T = sb("x1T", [P, EC, N])
        qT = sb("qT", [P, EC, GN])
        aT1 = sb("aT1", [P, EC, N])
        x3T = sb("x3T", [P, EC, N])
        mv = sb("mv", [P, 6])
        stats = sb("stats", [P, 6])
        mean = sb("mean", [P, 2])
        vare = sb("vare", [P, 1])
        rstd = sb("rstd", [P, 1])
        lam_p = sb("lam_p", [P, 2, D0])
        lam_e = sb("lam_e", [P, 2])
        neg_lam = sb("neg_lam", [P, 1])
        lnwb_s = sb("lnwb_s", [P, 2])

        pool_a = sb("pool_a", [P, EC * NX * N])
        pool_b = sb("pool_b", [P, FC * N])
        xm = pool_a[:, :].rearrange("p (c x n) -> p c x n", c=EC, x=NX)
        hT = pool_b[:, :].rearrange("p (c n) -> p c n", c=FC)
        patches_sb = pool_b[:, 0:PC * N].rearrange("p (c n) -> p c n", c=PC)
        km = pool_a[:, 0:EC * GB * HC * S].rearrange("p (c b h k) -> p c b h k", c=EC, b=GB, h=HC)
        prod = sb("prod", [P, 2, H0, H0, D0])
        prodv = prod[:, :, :, :, :].rearrange("p a n m d -> p (a n m d)").rearrange(
            "p (n e m) -> p n e m", n=H0, m=H0)
        qk = sb("qk", [P, 2 * E])
        qk_c = sb("qk_c", [P, 2 * E])
        qk_s = sb("qk_s", [P, 2 * E])
        v0 = sb("v0", [P, E])
        s0 = sb("s0", [P, 2, H0, H0])
        small = sb("small", [P, 4, 2, H0])
        amix = sb("amix", [P, H0, H0])
        att = sb("att", [P, E])
        attsq = sb("attsq", [P, E])
        ms = sb("ms", [P, 2, H0])
        attn_n = sb("attn_n", [P, E])
        aT = sb("aT", [P, EC, TT])

        x3 = sb("x3", [P, 2, 2, EC, KT, S])
        vb = sb("vb", [KR, 2, KC, 2, KT, VW])
        prob = sb("prob", [P, 2, EC, HC, S])
        smx = sb("smx", [P, 2, EC, HC])
        pT = sb("pT", [KR, 2, KC, P])
        oc = sb("oc", [P, 2, H1, VW])
        orc = sb("orc", [P, H1])
        on = sb("on", [P, 2, E])

        lmax = sb("lmax", [P, 1])
        lcand = sb("lcand", [P, NX])
        oh = sb("oh", [P, NX], BF16)
        ohT = sb("ohT", [NX, N])
        xbo = sb("xbo", [P, 2, E])
        hb = sb("hb", [P, 2, E])
        y = sb("y", [P, E])
        yo = sb("yo", [P, 2, E])

        d_patch = [sem(f"d_patch{t}") for t in range(NT)]
        d_tok, d_rows, d_sel = sem("d_tok"), sem("d_rows"), sem("d_sel")
        d_id, d_qkv, d_rope, d_small, d_w0, d_l1 = (
            sem("d_id"), sem("d_qkv"), sem("d_rope"), sem("d_small"), sem("d_w0"), sem("d_l1"))
        d_w1, d_tail = sem("d_w1"), sem("d_tail")
        d_out = [sem("d_out0"), sem("d_out1")]
        s_setup = sem("s_setup")
        dve_setup = sem("dve_setup")
        s_lam = sem("s_lam")
        s_lame = sem("s_lame")
        s_v = sem("s_v")
        s_p = sem("s_p")
        proj_done, h_ready = sem("proj_done"), sem("h_ready")
        var_ready, rstd_ready, xn_ready = sem("var_ready"), sem("rstd_ready"), sem("xn_ready")
        tp_done, tp_copied = sem("tp_done"), sem("tp_copied")
        qkv_done, qkv_copied = sem("qkv_done"), sem("qkv_copied")
        rope_s_ready, rope_ready, prod1_ready = sem("rope_s_ready"), sem("rope_ready"), sem("prod1_ready")
        s0_ready, p0_ready = sem("s0_ready"), sem("p0_ready")
        amix_ready, prodv_ready = sem("amix_ready"), sem("prodv_ready")
        att_ready, sq_ready, ms_ready, rms_ready = sem("att_ready"), sem("sq_ready"), sem("ms_ready"), sem("rms_ready")
        attn_ready = sem("attn_ready")
        acc_done, acc_added = sem("acc_done"), sem("acc_added")
        qk1_done, qk1_copied = sem("qk1_done"), sem("qk1_copied")
        x3_ready = sem("x3_ready")
        v1_done, v1_copied = sem("v1_done"), sem("v1_copied")
        s1_done, s1_sub, p1_ready = sem("s1_done"), sem("s1_sub"), sem("p1_ready")
        pt_done, pt_copied_a, pt_copied_v = sem("pt_done"), sem("pt_copied_a"), sem("pt_copied_v")
        pv_done, pv_copied, on_ready = sem("pv_done"), sem("pv_copied"), sem("on_ready")
        ot_done, ot_copied = sem("ot_done"), sem("ot_copied")
        logit_done, oh_ready, ohb_done = sem("logit_done"), sem("oh_ready"), sem("ohb_done")
        xm_ready, ohT_copied = sem("xm_ready"), sem("ohT_copied")
        ff_done, ff_ready, y_done = sem("ff_done"), sem("ff_ready"), sem("y_done")
        xbo_ready, hb_ready, yo_ready, y_taken = sem("xbo_ready"), sem("hb_ready"), sem("yo_ready"), sem("y_taken")

        def tile_cols(t):
            return slice(t * TT, (t + 1) * TT)

        def pair_cols(p, i):
            b = 2 * p + i
            at = (b // GB) * GN + (b % GB) * S
            return slice(at, at + S)

        block = ctx.enter_context(nc.Block())

        @block.sync
        def _(sp):
            sp.dma_start(tok_w_sb[:], tok_w).then_inc(d_tok, 16)
            sp.dma_start(patches_sb[:, :, tile_cols(0)], patches[:, :, tile_cols(0)]).then_inc(d_patch[0], 16)
            sp.dma_start(rows_sb[:], rows).then_inc(d_rows, 16)
            sp.dma_start(sel_sb[:], sel).then_inc(d_sel, 16)
            sp.dma_start(ident[:], ident_in).then_inc(d_id, 16)
            sp.dma_start(wqkv_sb[:], wqkv).then_inc(d_qkv, 16)
            sp.dma_start(rope_sb[0:TT], rope).then_inc(d_rope, 16)
            for dst, src in ((lam_sb, lam), (lnwb_sb, lnwb), (hmask_sb, hmask), (vmask_sb, vmask),
                             (causal_f, causal), (rowsel_f, rowsel), (disha_sb, disha)):
                sp.dma_start(dst[:], src).then_inc(d_small, 16)
            sp.dma_start(wo0_sb[:], wo0).then_inc(d_w0, 16)
            sp.dma_start(wf_sb[:], wf).then_inc(d_w0, 16)
            for t in range(1, NT):
                sp.dma_start(patches_sb[:, :, tile_cols(t)], patches[:, :, tile_cols(t)]).then_inc(d_patch[t], 16)
            for dst, src in ((wq1_sb, wq1), (wk1_sb, wk1), (wv1_sb, wv1), (wo1_sb, wo1), (vb, vones),
                             (wr_sb, wr), (b1_sb, b1)):
                sp.dma_start(dst[:], src).then_inc(d_l1, 16)
            sp.dma_start(w1_sb[:], w1).then_inc(d_w1, 16)
            sp.dma_start(wo2_sb[:], wo2).then_inc(d_w1, 16)
            sp.dma_start(tail_sb[:], tail).then_inc(d_tail, 16)
            for t in range(NT):
                sp.wait_ge(yo_ready, t + 1)
                sp.dma_start(out[tile_cols(t), :], yo[0:TT, t % 2, :]).then_inc(d_out[t % 2], 16)
            sp.wait_ge(d_out[0], 16 * (NT // 2))
            sp.wait_ge(d_out[1], 16 * (NT // 2))

        @block.tensor
        def _(pe):
            mm = nc.tensor.matmul

            def transposed(src, n, rows_=TT, cols=TT):
                if n:
                    pe.wait_ge(tp_copied, n)
                for c in range(EC):
                    last = nc.tensor.transpose(bank[4][:, c * P:c * P + rows_],
                                               src[0:rows_, c * P:(c + 1) * P], ident[0:rows_, 0:rows_])
                last.then_inc(tp_done, 1)

            def project(t):
                pe.wait_ge(d_patch[t], 16)
                if t:
                    pe.wait_ge(h_ready, t)
                for c in range(PC):
                    mm(bank[2][0:TT, 0:E], patches_sb[:, c, tile_cols(t)], tok_w_sb[:, c, :],
                       start=(c == 0), stop=False)
                mm(bank[2][0:TT, 0:E], sel_sb[:, tile_cols(t)], rows_sb[:, :],
                   start=False, stop=True).then_inc(proj_done, 1)

            for s_, n in ((d_tok, 16), (d_rows, 16), (d_sel, 16)):
                pe.wait_ge(s_, n)
            project(0)
            pe.wait_ge(d_id, 16)
            pe.wait_ge(d_qkv, 16)
            for t in range(NT):
                pe.wait_ge(xn_ready, 3 * t + 1)
                transposed(xn[:, t, :], 4 * t)
                pe.wait_ge(tp_copied, 4 * t + 1)
                if t:
                    pe.wait_ge(qkv_copied, 2 * t)
                for c in range(EC):
                    mm(bank[0][0:TT, :], xT[:, c, :], wqkv_sb[:, c, 0:2 * E], start=(c == 0), stop=(c == EC - 1))
                for c in range(EC):
                    last = mm(bank[1][0:TT, 0:E], xT[:, c, :], wqkv_sb[:, c, 2 * E:3 * E],
                              start=(c == 0), stop=(c == EC - 1))
                last.then_inc(qkv_done, 1)
                if t + 1 < NT:
                    project(t + 1)
                pe.wait_ge(attn_ready, t + 1)
                transposed(attn_n, 4 * t + 1)
                pe.wait_ge(tp_copied, 4 * t + 2)
                if t:
                    pe.wait_ge(acc_added, 2 * t)
                else:
                    pe.wait_ge(d_w0, 32)
                    pe.wait_ge(s_setup, 1)
                for c in range(EC):
                    last = mm(bank[3][0:TT, 0:E], aT[:, c, :], wo0_sb[:, c, :], start=(c == 0), stop=(c == EC - 1))
                last.then_inc(acc_done, 1)
                pe.wait_ge(xn_ready, 3 * t + 2)
                transposed(xn[:, t, :], 4 * t + 2)
                pe.wait_ge(tp_copied, 4 * t + 3)
                pe.wait_ge(acc_added, 2 * t + 1)
                for c in range(EC):
                    last = mm(bank[3][0:TT, 0:E], xT[:, c, :], wf_sb[:, c, :], start=(c == 0), stop=(c == EC - 1))
                last.then_inc(acc_done, 1)
                pe.wait_ge(xn_ready, 3 * t + 3)
                transposed(xn[:, t, :], 4 * t + 3)

            pe.wait_ge(tp_copied, 4 * NT)
            pe.wait_ge(acc_added, 2 * NT)
            pe.wait_ge(d_l1, 16 * 7)

            def qk_group(g):
                for i in range(2 * EC):
                    w, c_out = (wq1_sb, i) if i < EC else (wk1_sb, i - EC)
                    n = 2 * EC * g + i
                    if n >= 2:
                        pe.wait_ge(qk1_copied, n - 1)
                    for c in range(EC):
                        last = mm(bank[5 + i % 2][:, 0:GN], w[:, c, c_out * P:(c_out + 1) * P],
                                  x1T[:, c, g * GN:(g + 1) * GN], start=(c == 0), stop=(c == EC - 1))
                    last.then_inc(qk1_done, 1)

            def values(p):
                pe.wait_ge(x3_ready, p + 1)
                if p:
                    pe.wait_ge(v1_copied, p)
                for i in range(2):
                    for c in range(EC):
                        last = mm(bank[7][0:KR, i * E:(i + 1) * E],
                                  x3[:, p % 2, i, c, :, :].rearrange("p j k -> p (j k)"), wv1_sb[:, c, :],
                                  start=(c == 0), stop=(c == EC - 1))
                last.then_inc(v1_done, 1)

            def scores(p):
                if p:
                    pe.wait_ge(s1_sub, p)
                for c in range(EC):
                    o = bank[c][:, 0:HC * S]
                    mm(o, rowsel_sb[:, :], causal_sb[:, :].unsqueeze(1).to_broadcast([S, HC, S]),
                       start=True, stop=False, skip_group_check=True)
                    for i in range(2):
                        b = (2 * p + i) % GB
                        last = mm(bank[c][HALF * i:HALF * i + S, 0:HC * S], qT[:, c, b * S:(b + 1) * S],
                                  km[:, c, b, :, :], start=False, stop=(i == 1), skip_group_check=True)
                last.then_inc(s1_done, 1)

            def pt_out(c):
                return bank[2 + c // 4][:, (c % 4) * P:(c % 4 + 1) * P]

            def pv_out(c):
                return bank[5 + c // 4][0:HALF + S, (c % 4) * 2 * KT * VW:(c % 4 + 1) * 2 * KT * VW]

            def finish_pair(p):
                pe.wait_ge(p1_ready, p + 1)
                if p:
                    pe.wait_ge(pt_copied_a, p)
                    pe.wait_ge(pt_copied_v, p)
                pf = prob[:, p % 2, :, :, :].rearrange("p c h k -> p (c h k)")
                for c in range(KC):
                    r = KR if c < KC - 1 else S
                    last = nc.tensor.transpose(pt_out(c)[0:r, :], pf[:, c * KR:c * KR + r], ident[:, :])
                last.then_inc(pt_done, 1)
                pe.wait_ge(pt_copied_a, p + 1)
                pe.wait_ge(pt_copied_v, p + 1)
                pe.wait_ge(v1_copied, p + 1)
                if p:
                    pe.wait_ge(pv_copied, p)
                for c in range(KC):
                    r, w = (KR, KT * VW) if c < KC - 1 else (S, VW)
                    o = pv_out(c).rearrange("p (i w) -> p i w", i=2)[:, :, 0:w]
                    last = mm(o, pT[0:r, p % 2, c, 0:HALF + S],
                              vb[0:r, p % 2, c, :, :, :].rearrange("p i j w -> p i (j w)")[:, :, 0:w],
                              start=True, stop=True)
                last.then_inc(pv_done, 1)
                pe.wait_ge(on_ready, p + 1)
                if p:
                    pe.wait_ge(ot_copied, p)
                for c in range(EC):
                    last = nc.tensor.transpose(bank[4][:, c * P:(c + 1) * P], on[:, p % 2, c * P:(c + 1) * P],
                                               ident[:, :])
                last.then_inc(ot_done, 1)

            for g in range(G):
                if g:
                    pe.wait_ge(pv_copied, g * PAIRS // G)
                qk_group(g)
                pe.wait_ge(qk1_copied, 2 * EC * (g + 1))
                first = g * PAIRS // G
                scores(first)
                values(first)
                for p in range(first, first + PAIRS // G):
                    if p + 1 < first + PAIRS // G:
                        scores(p + 1)
                        values(p + 1)
                    finish_pair(p)

            pe.wait_ge(ot_copied, PAIRS)
            pe.wait_ge(d_w1, 32)

            def route(t):
                if t:
                    pe.wait_ge(acc_added, 2 * NT + t)
                for c in range(EC):
                    last = mm(bank[3][0:TT, 0:E], aT1[:, c, tile_cols(t)], wo1_sb[:, c, :],
                              start=(c == 0), stop=(c == EC - 1))
                last.then_inc(acc_done, 1)
                pe.wait_ge(xn_ready, 3 * NT + t + 1)
                transposed(xn[:, t, :], 4 * NT + t)
                pe.wait_ge(tp_copied, 4 * NT + t + 1)
                if t:
                    pe.wait_ge(oh_ready, t)
                for c in range(EC):
                    last = mm(bank[5][0:TT, 0:NX], x3T[:, c, tile_cols(t)], wr_sb[:, c, :],
                              start=(c == 0), stop=(c == EC - 1))
                last.then_inc(logit_done, 1)
                pe.wait_ge(oh_ready, t + 1)
                if t:
                    pe.wait_ge(xm_ready, t)
                    pe.wait_ge(ohT_copied, t)
                for e in range(NX):
                    mm(bank[6][:, e * TT:(e + 1) * TT], oh[0:TT, e:e + 1].to_broadcast([TT, P]),
                       identb[0:TT, 0:TT], start=True, stop=True)
                mm(bank[7][0:NX, 0:TT], oh[0:TT, :], identb[0:TT, 0:TT], start=True, stop=True).then_inc(ohb_done, 1)

            def experts(g):
                pe.wait_ge(xm_ready, GT * (g + 1))
                pe.wait_ge(ohT_copied, GT * (g + 1))
                cols = slice(g * GN, (g + 1) * GN)
                for f in range(FC):
                    n = g * FC + f
                    if n >= 2:
                        pe.wait_ge(ff_ready, n - 1)
                    o = bank[n % 2][:, 0:GN]
                    for e in range(NX):
                        for c in range(EC):
                            mm(o, w1_sb[:, c, e, f * P:(f + 1) * P], xm[:, c, e, cols],
                               start=(e == 0 and c == 0), stop=False)
                    mm(o, b1_sb[:, f * P:(f + 1) * P], ohT[:, cols], start=False, stop=True).then_inc(ff_done, 1)

            def down(t):
                pe.wait_ge(ff_ready, FC * (t // GT + 1))
                if t:
                    pe.wait_ge(y_taken, t)
                for f in range(FC):
                    last = mm(bank[2][0:TT, 0:E], hT[:, f, tile_cols(t)], wo2_sb[:, f, :],
                              start=(f == 0), stop=(f == FC - 1))
                last.then_inc(y_done, 1)

            for t in range(GT):
                route(t)
            experts(0)
            for t in range(GT, NT):
                route(t)
            for t in range(GT):
                down(t)
            experts(1)
            for t in range(GT, NT):
                down(t)

        @block.scalar
        def _(act):
            fn = nc.scalar.activation

            def turn_out(n, dst):
                act.wait_ge(tp_done, n + 1)
                fn(dst, bank[4][:, 0:EC * P].rearrange("p (c n) -> p c n", c=EC)[:, :, 0:TT],
                   ACT.Copy).then_inc(tp_copied, 1)

            act.wait_ge(s_lam, 1)
            fn(lam_e[:, :], lam_e[:, :], ACT.Exp).then_inc(s_lame, 1)

            def h_copy(t):
                act.wait_ge(proj_done, t + 1)
                fn(h[0:TT, t, :], bank[2][0:TT, 0:E], ACT.Copy).then_inc(h_ready, 1)

            h_copy(0)
            act.wait_ge(dve_setup, 1)
            for t in range(NT):
                turn_out(4 * t, xT[:, :, :])
                act.wait_ge(qkv_done, t + 1)
                if t:
                    act.wait_ge(prod1_ready, t)
                    act.wait_ge(prodv_ready, t)
                fn(qk[0:TT, :], bank[0][0:TT, :], ACT.Copy).then_inc(qkv_copied, 1)
                fn(v0[0:TT, :], bank[1][0:TT, 0:E], ACT.Copy).then_inc(qkv_copied, 1)
                if t + 1 < NT:
                    h_copy(t + 1)
                act.wait_ge(s0_ready, t + 1)
                fn(s0[0:TT], s0[0:TT], ACT.Exp, scale=SCALE0).then_inc(p0_ready, 1)
                act.wait_ge(att_ready, t + 1)
                fn(attsq[0:TT, :], att[0:TT, :], ACT.Square).then_inc(sq_ready, 1)
                act.wait_ge(tp_done, 4 * t + 2)
                fn(aT[:, :, :], bank[4][:, 0:EC * P].rearrange("p (c n) -> p c n", c=EC)[:, :, 0:TT],
                   ACT.Identity, scale=lnwb_s[:, 0:1], bias=lnwb_s[:, 1:2]).then_inc(tp_copied, 1)
                turn_out(4 * t + 2, xT[:, :, :])
                turn_out(4 * t + 3, x1T[:, :, tile_cols(t)])

            def qk_group(g):
                for i in range(2 * EC):
                    act.wait_ge(qk1_done, 2 * EC * g + i + 1)
                    if i < EC:
                        fn(qT[:, i, :], bank[5 + i % 2][:, 0:GN], ACT.Copy).then_inc(qk1_copied, 1)
                        continue
                    src = bank[5 + i % 2][:, 0:GB * S].rearrange("p (b k) -> p b k", b=GB)
                    for j in range(HC):
                        last = fn(km[:, i - EC, :, j, :], src, ACT.Copy, scale=hmask_sb[:, j:j + 1])
                    last.then_inc(qk1_copied, 1)

            def probs(p):
                act.wait_ge(s1_sub, p + 1)
                x = prob[:, p % 2, :, :, :]
                fn(x, x, ACT.Exp, scale=SCALE1).then_inc(p1_ready, 1)

            def finish_pair(p):
                act.wait_ge(pt_done, p + 1)
                if p >= 2:
                    act.wait_ge(pv_done, p - 1)
                fn(pT[:, p % 2, 0:4, :], bank[2][0:KR, :].rearrange("p (c n) -> p c n", c=4),
                   ACT.Copy).then_inc(pt_copied_a, 1)
                act.wait_ge(pv_done, p + 1)
                if p >= 2:
                    act.wait_ge(on_ready, p - 1)
                for i in range(2):
                    rows_ = slice(HALF * i, HALF * i + S)
                    o = bank[5][rows_, 0:8 * KT * VW].rearrange("p (c i w) -> p c i w", c=4, i=2)
                    fn(oc[rows_, p % 2, 0:4 * KT, :].rearrange("p (c j) w -> p c (j w)", c=4), o[:, :, i, :], ACT.Copy)
                    at = i * KT * VW
                    fn(oc[rows_, p % 2, 4 * KT:5 * KT, :].rearrange("p j w -> p (j w)"),
                       bank[6][rows_, at:at + KT * VW], ACT.Copy)
                    at += 2 * KT * VW
                    last = fn(oc[rows_, p % 2, 5 * KT, :], bank[6][rows_, at:at + VW], ACT.Copy)
                last.then_inc(pv_copied, 1)
                act.wait_ge(ot_done, p + 1)
                at = pair_cols(p, 0).start
                fn(aT1[:, :, at:at + 2 * S].rearrange("p c (i n) -> p c i n", i=2),
                   bank[4][:, 0:EC * P].rearrange("p (c i n) -> p c i n", c=EC, i=2)[:, :, :, 0:S],
                   ACT.Copy).then_inc(ot_copied, 1)

            act.wait_ge(d_small, 16 * 7)
            for g in range(G):
                if g:
                    act.wait_ge(s1_done, g * PAIRS // G)
                qk_group(g)
                first = g * PAIRS // G
                probs(first)
                for p in range(first, first + PAIRS // G):
                    if p + 1 < first + PAIRS // G:
                        probs(p + 1)
                    finish_pair(p)

            def route(t):
                turn_out(4 * NT + t, x3T[:, :, tile_cols(t)])
                act.wait_ge(ohb_done, t + 1)
                fn(ohT[:, tile_cols(t)], bank[7][0:NX, 0:TT], ACT.Copy).then_inc(ohT_copied, 1)

            def experts(g):
                for f in range(FC):
                    n = g * FC + f
                    act.wait_ge(ff_done, n + 1)
                    fn(hT[:, f, g * GN:(g + 1) * GN], bank[n % 2][:, 0:GN], ACT.Gelu).then_inc(ff_ready, 1)

            for t in range(GT):
                route(t)
            experts(0)
            for t in range(GT, NT):
                route(t)
            experts(1)

        @block.vector
        def _(dve):
            tt, ts, red = nc.vector.tensor_tensor, nc.vector.tensor_scalar, nc.vector.tensor_reduce
            count = [0]

            def step(ins):
                count[0] += 1
                ins.then_inc(s_v, 1)
                dve.wait_ge(s_v, count[0])

            def norm(n, src, dst, eps):
                step(nc.vector.bn_stats(stats[0:TT, :], src))
                step(nc.vector.bn_aggr(mean[0:TT, :], stats[0:TT, :]))
                ts(vare[0:TT, :], mean[0:TT, 1:2], eps, None, ALU.add).then_inc(var_ready, 1)
                dve.wait_ge(rstd_ready, n + 1)
                return ts(dst, src, mean[0:TT, 0:1], rstd[0:TT, :], ALU.subtract, ALU.mult)

            dve.wait_ge(d_small, 16 * 7)
            step(tt(lam_p[:], lam_sb[:, :, 0, :], lam_sb[:, :, 1, :], ALU.mult))
            red(lam_e[:, :], lam_p[:], AX, ALU.add).then_inc(s_lam, 1)
            step(ts(lnwb_s[:, :], lnwb_sb[:, :], 1.0 - LAMBDA_INIT, None, ALU.mult))
            dve.wait_ge(s_lame, 1)
            step(tt(neg_lam[:], lam_e[:, 1:2], lam_e[:, 0:1], ALU.subtract))
            step(ts(neg_lam[:], neg_lam[:], -LAMBDA_INIT, None, ALU.add))
            nc.vector.memset(oc[:], 1.0).then_inc(dve_setup, 1)
            dve.wait_ge(d_rope, 16)

            r = slice(0, TT)
            for t in range(NT):
                dve.wait_ge(h_ready, t + 1)
                norm(3 * t, h[r, t, :], xn[r, t, :], LN_EPS).then_inc(xn_ready, 1)
                dve.wait_ge(qkv_copied, 2 * t + 2)
                cos = rope_sb[r, t, 0, :].unsqueeze(1).to_broadcast([TT, 4 * H0, D0])
                x = qk[r, :].rearrange("p (g d) -> p g d", d=D0)
                xc = qk_c[r, :].rearrange("p (g d) -> p g d", d=D0)
                step(tt(xc, x, cos, ALU.mult))
                dve.wait_ge(rope_s_ready, t + 1)
                tt(qk_c[r, :], qk_c[r, :], qk_s[r, :], ALU.add).then_inc(rope_ready, 1)
                dve.wait_ge(rope_ready, t + 1)
                q = qk_c[r, 0:E].rearrange("p (n a d) -> p n a d", n=H0, a=2)
                k = qk_c[r, E:2 * E].rearrange("p (n a d) -> p n a d", n=H0, a=2)
                step(tt(prod[r, 0], q[:, :, 0, :].unsqueeze(2).to_broadcast([TT, H0, H0, D0]),
                        k[:, :, 0, :].unsqueeze(1).to_broadcast([TT, H0, H0, D0]), ALU.mult))
                step(red(s0[r, 0], prod[r, 0], AX, ALU.add))
                dve.wait_ge(prod1_ready, t + 1)
                step(red(s0[r, 1], prod[r, 1], AX, ALU.add))
                mx, sm, rc, wt = (small[r, i] for i in range(4))
                step(red(mx, s0[r], AX, ALU.max))
                tt(s0[r], s0[r], mx.unsqueeze(3).to_broadcast([TT, 2, H0, H0]), ALU.subtract).then_inc(s0_ready, 1)
                dve.wait_ge(p0_ready, t + 1)
                step(red(sm, s0[r], AX, ALU.add))
                step(nc.vector.reciprocal(rc, sm))
                step(ts(rc[:, 1, :], rc[:, 1, :], neg_lam[r, :], None, ALU.mult))
                step(tt(s0[r], s0[r], rc.unsqueeze(3).to_broadcast([TT, 2, H0, H0]), ALU.mult))
                tt(amix[r], s0[r, 0], s0[r, 1], ALU.add).then_inc(amix_ready, 1)
                dve.wait_ge(amix_ready, t + 1)
                nv = 5
                step(tt(prodv[r, 0:nv], amix[r, 0:nv].unsqueeze(2).to_broadcast([TT, nv, 2 * D0, H0]),
                        v0[r, :].rearrange("p (m e) -> p e m", m=H0).unsqueeze(1).to_broadcast([TT, nv, 2 * D0, H0]),
                        ALU.mult))
                av = att[r, :].rearrange("p (n e) -> p n e", n=H0)
                red(av[:, 0:nv, :], prodv[r, 0:nv], AX, ALU.add)
                dve.wait_ge(prodv_ready, t + 1)
                red(av[:, nv:H0, :], prodv[r, nv:H0], AX, ALU.add).then_inc(att_ready, 1)
                dve.wait_ge(sq_ready, t + 1)
                step(red(ms[r, 0, :], attsq[r, :].rearrange("p (n e) -> p n e", n=H0), AX, ALU.add))
                ts(ms[r, 0, :], ms[r, 0, :], 1.0 / (2 * D0), RMS_EPS, ALU.mult, ALU.add).then_inc(ms_ready, 1)
                dve.wait_ge(rms_ready, t + 1)
                tt(attn_n[r, :].rearrange("p (n e) -> p n e", n=H0), av,
                   ms[r, 1, :].unsqueeze(2).to_broadcast([TT, H0, 2 * D0]), ALU.mult).then_inc(attn_ready, 1)
                for i in range(2):
                    dve.wait_ge(acc_done, 2 * t + i + 1)
                    tt(h[r, t, :], h[r, t, :], bank[3][r, 0:E], ALU.add).then_inc(acc_added, 1)
                    dve.wait_ge(acc_added, 2 * t + i + 1)
                    norm(3 * t + 1 + i, h[r, t, :], xn[r, t, :], LN_EPS).then_inc(xn_ready, 1)

            dve.wait_ge(d_l1, 16 * 7)

            def softmax_in(p):
                dve.wait_ge(s1_done, p + 1)
                if p >= 2:
                    dve.wait_ge(pt_done, p - 1)
                for c in range(EC):
                    sc = bank[c][:, 0:HC * S].rearrange("p (h k) -> p h k", h=HC)
                    m = smx[:, p % 2, c, :]
                    step(red(m, sc, AX, ALU.max))
                    last = tt(prob[:, p % 2, c], sc, m.unsqueeze(2).to_broadcast([P, HC, S]), ALU.subtract)
                last.then_inc(s1_sub, 1)

            def values(p):
                dve.wait_ge(v1_done, p + 1)
                if p >= 2:
                    dve.wait_ge(pv_done, p - 1)
                nf = KC - 1
                for i in range(2):
                    src = bank[7][0:KR, i * E:i * E + nf * KT * D1].rearrange("p (c j e) -> p c j e", c=nf, j=KT)
                    for j in range(KT):
                        tt(vb[:, p % 2, 0:nf, i, j, 0:D1], src[:, :, j, :],
                           vmask_sb[:, j, :].unsqueeze(1).to_broadcast([KR, nf, D1]), ALU.mult)
                    last = nc.vector.tensor_copy(vb[0:S, p % 2, nf, i, 0, 0:D1],
                                                 bank[7][0:S, i * E + nf * KT * D1:(i + 1) * E])
                last.then_inc(v1_copied, 1)

            def finish_pair(p):
                dve.wait_ge(pt_done, p + 1)
                nc.vector.tensor_copy(pT[:, p % 2, 4, :], bank[3][0:KR, 0:P])
                nc.vector.tensor_copy(pT[0:S, p % 2, 5, :], bank[3][0:S, P:2 * P]).then_inc(pt_copied_v, 1)
                dve.wait_ge(pv_copied, p + 1)
                if p >= 2:
                    dve.wait_ge(ot_done, p - 1)
                step(nc.vector.reciprocal(orc[:, :], oc[:, p % 2, :, D1]))
                tt(on[:, p % 2, :].rearrange("p (h e) -> p h e", h=H1), oc[:, p % 2, :, 0:D1],
                   orc[:, :].unsqueeze(2).to_broadcast([P, H1, D1]), ALU.mult).then_inc(on_ready, 1)

            for g in range(G):
                first = g * PAIRS // G
                softmax_in(first)
                values(first)
                for p in range(first, first + PAIRS // G):
                    if p + 1 < first + PAIRS // G:
                        softmax_in(p + 1)
                        values(p + 1)
                    finish_pair(p)

            dve.wait_ge(d_tail, 16)

            def route(t):
                dve.wait_ge(acc_done, 2 * NT + t + 1)
                tt(h[r, t, :], h[r, t, :], bank[3][r, 0:E], ALU.add).then_inc(acc_added, 1)
                dve.wait_ge(acc_added, 2 * NT + t + 1)
                norm(3 * NT + t, h[r, t, :], xn[r, t, :], LN_EPS).then_inc(xn_ready, 1)
                dve.wait_ge(logit_done, t + 1)
                step(red(lmax[r, :], bank[5][r, 0:NX], AX, ALU.max))
                step(nc.vector.scalar_tensor_tensor(out=lcand[r, :], in0=bank[5][r, 0:NX], scalar=lmax[r, :],
                                                    in1=tie_sb[r, :], op0=ALU.is_equal, op1=ALU.mult))
                step(red(lmax[r, :], lcand[r, :], AX, ALU.max))
                ts(oh[r, :], lcand[r, :], lmax[r, :], None, ALU.is_equal).then_inc(oh_ready, 1)
                dve.wait_ge(ohb_done, t + 1)
                for c in range(EC):
                    last = tt(xm[:, c, :, tile_cols(t)],
                              bank[6][:, 0:NX * TT].rearrange("p (x n) -> p x n", x=NX),
                              x3T[:, c, tile_cols(t)].unsqueeze(1).to_broadcast([P, NX, TT]), ALU.mult)
                last.then_inc(xm_ready, 1)

            def finish(t):
                dve.wait_ge(y_done, t + 1)
                dve.wait_ge(xbo_ready, t + 1)
                if t:
                    dve.wait_ge(yo_ready, t)
                tt(y[r, :], bank[2][r, 0:E], xbo[r, t % 2, :], ALU.add).then_inc(y_taken, 1)
                dve.wait_ge(y_taken, t + 1)
                step(norm(4 * NT + t, y[r, :], y[r, :], LN_EPS_OUT))
                step(tt(y[r, :], y[r, :], gamma_sb[r, :], ALU.mult))
                dve.wait_ge(hb_ready, t + 1)
                if t >= 2:
                    dve.wait_ge(d_out[t % 2], 16 * (t // 2))
                tt(yo[r, t % 2, :], y[r, :], hb[r, t % 2, :], ALU.add).then_inc(yo_ready, 1)

            for t in range(NT):
                route(t)
            for t in range(NT):
                finish(t)

        @block.gpsimd
        def _(pool):
            tt = nc.gpsimd.tensor_tensor
            r = slice(0, TT)
            nc.gpsimd.memset(expo[:, :], -0.5).then_inc(s_p, 1)
            for g in range(G):
                nc.gpsimd.memset(aT1[:, :, g * GN + GB * S:(g + 1) * GN], 0.0)
            pool.wait_ge(d_id, 16)
            nc.gpsimd.tensor_copy(identb[:, :], ident[:, :])
            pool.wait_ge(d_small, 16 * 7)
            nc.gpsimd.tensor_copy(causal_sb[:, :], causal_f[:, :])
            nc.gpsimd.tensor_copy(rowsel_sb[:, :], rowsel_f[:, :])
            pool.wait_ge(d_w0, 32)
            tt(wf_sb[:], wf_sb[:], disha_sb[:, :].unsqueeze(1).to_broadcast([P, EC, E]), ALU.add).then_inc(s_setup, 1)
            pool.wait_ge(s_p, 1)

            def power(n):
                pool.wait_ge(var_ready, n + 1)
                tt(rstd[r, :], vare[r, :], expo[r, 0:1], ALU.pow).then_inc(rstd_ready, 1)

            for t in range(NT):
                power(3 * t)
                pool.wait_ge(qkv_copied, 2 * t + 1)
                if t == 0:
                    pool.wait_ge(d_rope, 16)
                if t:
                    pool.wait_ge(rope_ready, t)
                half = D0 // 2
                x = qk[r, :].rearrange("p (g a d) -> p g a d", a=2, d=half)
                xs = qk_s[r, :].rearrange("p (g a d) -> p g a d", a=2, d=half)
                for a in range(2):
                    sin = rope_sb[r, t, 1, a * half:(a + 1) * half].unsqueeze(1).to_broadcast([TT, 4 * H0, half])
                    last = tt(xs[:, :, a, :], x[:, :, 1 - a, :], sin, ALU.mult)
                last.then_inc(rope_s_ready, 1)
                pool.wait_ge(rope_ready, t + 1)
                q = qk_c[r, 0:E].rearrange("p (n a d) -> p n a d", n=H0, a=2)
                k = qk_c[r, E:2 * E].rearrange("p (n a d) -> p n a d", n=H0, a=2)
                tt(prod[r, 1], q[:, :, 1, :].unsqueeze(2).to_broadcast([TT, H0, H0, D0]),
                   k[:, :, 1, :].unsqueeze(1).to_broadcast([TT, H0, H0, D0]), ALU.mult).then_inc(prod1_ready, 1)
                pool.wait_ge(amix_ready, t + 1)
                nv = 5
                tt(prodv[r, nv:H0], amix[r, nv:H0].unsqueeze(2).to_broadcast([TT, H0 - nv, 2 * D0, H0]),
                   v0[r, :].rearrange("p (m e) -> p e m", m=H0).unsqueeze(1).to_broadcast([TT, H0 - nv, 2 * D0, H0]),
                   ALU.mult).then_inc(prodv_ready, 1)
                pool.wait_ge(ms_ready, t + 1)
                tt(ms[r, 1, :], ms[r, 0, :], expo[r, 0:H0], ALU.pow).then_inc(rms_ready, 1)
                power(3 * t + 1)
                power(3 * t + 2)

            pool.wait_ge(tp_copied, 4 * NT)
            for p in range(PAIRS):
                if p >= 2:
                    pool.wait_ge(v1_done, p - 1)
                for i in range(2):
                    for c in range(EC):
                        last = nc.gpsimd.tensor_copy(
                            x3[:, p % 2, i, c],
                            x1T[:, c, pair_cols(p, i)].unsqueeze(1).to_broadcast([P, KT, S]))
                last.then_inc(x3_ready, 1)

            pool.wait_ge(d_tail, 16)

            def residual(t):
                pool.wait_ge(xn_ready, 3 * NT + t + 1)
                if t >= 2:
                    pool.wait_ge(yo_ready, t - 1)
                tt(xbo[r, t % 2, :], xn[r, t, :], bo_sb[r, :], ALU.add).then_inc(xbo_ready, 1)
                tt(hb[r, t % 2, :], h[r, t, :], beta_sb[r, :], ALU.add).then_inc(hb_ready, 1)

            for t in range(NT):
                power(3 * NT + t)
            for t in range(NT):
                residual(t)
                power(4 * NT + t)


def rope_tables():
    inv = (1.0 / np.float32(10000.0) ** (np.arange(0, D0, 2, dtype=np.float32) / np.float32(D0))).astype(np.float32)
    slot = np.arange(N) % GN
    pos = (slot % S).astype(np.float32)
    f = pos[:, None] * inv[None, :]
    cos, sin = np.cos(f), np.sin(f)
    t = np.stack([np.concatenate([cos, cos], 1), np.concatenate([-sin, sin], 1)], 1).astype(np.float32)
    return np.ascontiguousarray(t.reshape(NT, TT, 2, D0).transpose(1, 0, 2, 3))


def kernel(x, cls_tok, L0_tok_W, L0_tok_b, L0_tok_cls_token, L0_tok_pos_embed, L0_attn_Wq, L0_attn_Wk,
           L0_attn_Wv, L0_attn_Wo, L0_attn_lambda_q1, L0_attn_lambda_k1, L0_attn_lambda_q2,
           L0_attn_lambda_k2, L0_attn_ln_w, L0_attn_ln_b, L0_ffn_weight, L0_ffn_disha, L1_attn_q_proj,
           L1_attn_k_proj, L1_attn_v_proj, L1_attn_o_proj, L1_ffn_W_router, L1_ffn_W1, L1_ffn_b1,
           L1_ffn_Wo, L1_ffn_bo, L1_ffn_ln_gamma, L1_ffn_ln_beta):
    from concourse import bacc
    from concourse.bass_utils import run_bass_kernel_spmd

    a = np.asarray

    def chunks(w):
        w = a(w)
        return np.ascontiguousarray(w.reshape(w.shape[0] // P, P, w.shape[1]).transpose(1, 0, 2))

    def tiled(v, reps):
        return np.concatenate([a(v)] * reps, axis=0)

    pt = a(x).reshape(B, CIN, NP, PATCH, NP, PATCH).transpose(0, 2, 4, 1, 3, 5).reshape(B, NP * NP, PD)
    slots = np.zeros((G, GN, PD), np.float32)
    for b in range(B):
        at = (b % GB) * S
        slots[b // GB, at + 2:at + S] = pt[b]
    patches = np.ascontiguousarray(slots.reshape(N, PC, P).transpose(2, 1, 0))
    sel = np.zeros((ROWS, N), np.float32)
    for g in range(G):
        for n in range(GB * S):
            s = n % S
            for row in ([0], [1, 3], [2, 3 + s - 1])[min(s, 2)]:
                sel[row, g * GN + n] = 1.0
    rows = np.concatenate([a(cls_tok).reshape(1, E), a(L0_tok_cls_token).reshape(1, E),
                           a(L0_tok_b).reshape(1, E), a(L0_tok_pos_embed).reshape(S - 1, E)], 0)
    order = np.arange(E).reshape(2 * H0, D0 // 2, 2).transpose(0, 2, 1).reshape(E)
    wqkv = chunks(np.concatenate([a(L0_attn_Wq)[:, order], a(L0_attn_Wk)[:, order], a(L0_attn_Wv)], 1))
    lam = np.stack([a(L0_attn_lambda_q1), a(L0_attn_lambda_k1), a(L0_attn_lambda_q2), a(L0_attn_lambda_k2)])
    lam = np.ascontiguousarray(np.broadcast_to(lam.reshape(1, 2, 2, D0), (P, 2, 2, D0)))
    lnwb = np.stack([tiled(L0_attn_ln_w, P // (2 * D0)), tiled(L0_attn_ln_b, P // (2 * D0))], 1)
    part = np.arange(P)
    hmask = (part[:, None] // D1 == np.arange(HC)[None, :]).astype(np.float32)
    vmask = np.zeros((KR, KT, D1), np.float32)
    vones = np.zeros((KR, 2, KC, 2, KT, VW), np.float32)
    for j in range(KT):
        vmask[j * S:(j + 1) * S, j] = 1.0
        vones[j * S:(j + 1) * S, :, :, :, j, D1] = 1.0
    causal = np.where(np.tril(np.ones((S, S), bool)), 0.0, MASKED).astype(np.float32)
    rowsel = (part[None, :] % HALF == np.arange(S)[:, None]).astype(np.float32)
    w1 = np.ascontiguousarray(a(L1_ffn_W1).reshape(NX, EC, P, FF).transpose(2, 1, 0, 3))
    tie = np.arange(NX, 0, -1).astype(np.float32)
    tail = np.concatenate([a(L1_ffn_bo), a(L1_ffn_ln_gamma), a(L1_ffn_ln_beta), tie])
    tail = np.ascontiguousarray(np.broadcast_to(tail[None, :], (P, tail.size)))

    arrays = {
        "patches": patches, "tok_w": chunks(a(L0_tok_W).T), "rows": rows, "sel": sel, "wqkv": wqkv,
        "rope": rope_tables(), "lam": lam, "lnwb": lnwb, "wo0": chunks(L0_attn_Wo),
        "wf": chunks(a(L0_ffn_weight).T), "disha": tiled(L0_ffn_disha, 2), "wq1": chunks(a(L1_attn_q_proj).T),
        "wk1": chunks(a(L1_attn_k_proj).T), "wv1": chunks(a(L1_attn_v_proj).T),
        "wo1": chunks(a(L1_attn_o_proj).T), "hmask": hmask, "vmask": vmask, "vones": vones,
        "causal": causal, "rowsel": rowsel, "ident": np.eye(P, dtype=np.float32), "wr": chunks(L1_ffn_W_router),
        "w1": w1, "b1": a(L1_ffn_b1), "wo2": chunks(L1_ffn_Wo), "tail": tail,
    }
    nc = bacc.Bacc("TRN2", target_bir_lowering=False, num_devices=1)
    named, args = {}, []
    for name, v in arrays.items():
        v = np.ascontiguousarray(v)
        named[f"in_{name}"] = v
        args.append(nc.dram_tensor(f"in_{name}", v.shape, mybir.dt.from_np(v.dtype), kind="ExternalInput").ap())
    args.append(nc.dram_tensor("out_0", (N, E), F32, kind="ExternalOutput").ap())
    tower_kernel(nc, *args)
    res = run_bass_kernel_spmd(nc, [named], core_ids=[0])
    got = a(res.results[0]["out_0"]).reshape(G, GN, E)[:, 0:GB * S].reshape(B, S, E)
    return np.ascontiguousarray(got)
```

```python
from contextlib import ExitStack
import math

import numpy as np
import concourse.bass as bass
from concourse import mybir

F32 = mybir.dt.float32
BF16 = mybir.dt.bfloat16
ALU = mybir.AluOpType
ACT = mybir.ActivationFunctionType
AX = mybir.AxisListType.X

P = 128
B, CIN, IMG, PATCH = 16, 3, 96, 16
NP = IMG // PATCH
PD = CIN * PATCH * PATCH
S = NP * NP + 2
E = 256
EC = E // P
PC = PD // P
G = 2
GB = B // G
TT = 102
GT = 3
GN = GT * TT
NT = G * GT
N = G * GN
H0, D0 = 8, 16
H1, D1 = 16, 16
HC = H1 // EC
KT = 3
KC = -(-H1 // KT)
KR = KT * S
VW = D1 + 1
NX = 4
FF = 1024
FC = FF // P
PAIRS = B // 2
HALF = 64
LAMBDA_INIT = 0.8 - 0.6 * math.exp(-0.3 * 12)
RMS_EPS, LN_EPS, LN_EPS_OUT = 1e-8, 1e-5, 1e-12
SCALE0 = 1.0 / D0 ** 0.25
SCALE1 = 1.0 / D1 ** 0.5
MASKED = -1e30
NORMS = 5
NV = 4
ROWS = 3 + NP * NP + 1


QK_EARLY = {GT + 1: (0, 1), GT + 2: (2,), GT + 3: (3,)}
QK_LATE = {0: (0, 1), 1: (2,), 2: (3,)}


def route_steps(slot):
    return [(i, slot - 2 * i) for i in range(GT) if 0 <= slot - 2 * i < 4]


def tower_kernel(nc, patches, tok_w, rows, sel, wqkv, rope, lam, lnwb, wo0, wf, disha, wq1, wk1, wv1,
                 wo1, hmask, vmask, vones, causal, rowsel, ident_in, wr, w1, b1, wo2, tail, out):
    with ExitStack() as ctx:
        def sb(name, shape, dt=F32):
            return ctx.enter_context(nc.sbuf_tensor(name, shape, dt))

        def sem(name):
            return ctx.enter_context(nc.semaphore(name))

        bank = [ctx.enter_context(nc.psum_tensor(f"bank{i}", [P, 512], F32)) for i in range(8)]

        tok_w_sb = sb("tok_w_sb", [P, PC, E])
        rows_sb = sb("rows_sb", [ROWS, E])
        sel_sb = sb("sel_sb", [ROWS, N])
        wqkv_sb = sb("wqkv_sb", [P, EC, 3 * E])
        rope_sb = sb("rope_sb", [P, NT, 2, D0])
        lam_sb = sb("lam_sb", [P, 2, 2, D0])
        lnwb_sb = sb("lnwb_sb", [P, 2])
        wo0_sb = sb("wo0_sb", [P, EC, E])
        wf_sb = sb("wf_sb", [P, EC, E])
        disha_sb = sb("disha_sb", [P, E])
        wq1_sb = sb("wq1_sb", [P, EC, E])
        wk1_sb = sb("wk1_sb", [P, EC, E])
        wv1_sb = sb("wv1_sb", [P, EC, E])
        wo1_sb = sb("wo1_sb", [P, EC, E])
        hmask_sb = sb("hmask_sb", [P, HC])
        vmask_sb = sb("vmask_sb", [KR, KT, D1])
        causal_f = sb("causal_f", [S, S])
        rowsel_f = sb("rowsel_f", [S, P])
        causal_sb = sb("causal_sb", [S, S], BF16)
        rowsel_sb = sb("rowsel_sb", [S, P], BF16)
        ident = sb("ident", [P, P])
        identb = sb("identb", [P, P], BF16)
        wr_sb = sb("wr_sb", [P, EC, NX])
        w1_sb = sb("w1_sb", [P, EC, NX, FF])
        b1_sb = sb("b1_sb", [NX, FF])
        wo2_sb = sb("wo2_sb", [P, FC, E])
        tail_sb = sb("tail_sb", [P, 3 * E + NX])
        bo_sb = tail_sb[:, 0:E]
        gamma_sb = tail_sb[:, E:2 * E]
        beta_sb = tail_sb[:, 2 * E:3 * E]
        tie_sb = tail_sb[:, 3 * E:3 * E + NX]
        expo = sb("expo", [P, 16])

        h = sb("h", [P, NT, E])
        xn = sb("xn", [P, NT, E])
        xT0 = sb("xT0", [P, EC, TT])
        xTf = sb("xTf", [P, EC, TT])
        x1T = sb("x1T", [P, EC, N])
        qT = sb("qT", [P, G, EC, GN])
        aT1 = sb("aT1", [P, EC, N])
        x3T = sb("x3T", [P, EC, N])
        stats = sb("stats", [P, NORMS, NT, 6])
        mean = sb("mean", [P, NORMS, NT, 2])
        vare = sb("vare", [P, NORMS, NT, 1])
        rstd = sb("rstd", [P, NORMS, NT, 1])
        lam_p = sb("lam_p", [P, 2, D0])
        lam_e = sb("lam_e", [P, 2])
        neg_lam = sb("neg_lam", [P, 1])
        lnwb_s = sb("lnwb_s", [P, 2])

        pool_a = sb("pool_a", [P, EC * NX * N])
        pool_b = sb("pool_b", [P, FC * N])
        xm = pool_a[:, :].rearrange("p (c x n) -> p c x n", c=EC, x=NX)
        hT = pool_b[:, :].rearrange("p (c n) -> p c n", c=FC)
        patches_sb = pool_b[:, 0:PC * N].rearrange("p (t c n) -> p t c n", t=NT, c=PC)
        km = [b[:, 0:EC * GB * HC * S].rearrange("p (c b h k) -> p c b h k", c=EC, b=GB, h=HC)
              for b in (pool_a, pool_b)]
        prod = sb("prod", [P, 2, H0, H0, D0])
        prodv = prod[:, :, :, :, :].rearrange("p a n m d -> p (a n m d)").rearrange(
            "p (n e m) -> p n e m", n=H0, m=H0)
        qk = sb("qk", [P, 2 * E])
        qk_c = sb("qk_c", [P, 2 * E])
        qk_s = sb("qk_s", [P, 2 * E])
        v0 = sb("v0", [P, 2, E])
        s0 = sb("s0", [P, 2, H0, H0])
        small = sb("small", [P, 4, 2, H0])
        amix = sb("amix", [P, H0, H0])
        att = sb("att", [P, E])
        attsq = sb("attsq", [P, E])
        ms = sb("ms", [P, 2, 2, H0])
        attn_n = sb("attn_n", [P, E])
        aT = sb("aT", [P, EC, TT])

        x3 = sb("x3", [P, 2, 2, EC, KT, S])
        vb = sb("vb", [KR, 2, KC, 2, KT, VW])
        prob = sb("prob", [P, 2, EC, HC, S])
        smx = sb("smx", [P, 2, EC, HC])
        pT = sb("pT", [KR, 2, KC, P])
        oc = sb("oc", [P, 2, H1, VW])
        orc = sb("orc", [P, H1])
        on = sb("on", [P, 2, E])

        lmax = sb("lmax", [P, 1])
        lcand = sb("lcand", [P, NX])
        oh = sb("oh", [P, 2, NX], BF16)
        ohT = sb("ohT", [NX, N])
        xbo = sb("xbo", [P, 2, E])
        hb = sb("hb", [P, 2, E])
        y = sb("y", [P, 2, E])
        yo = sb("yo", [P, 2, E])

        d_patch = [sem(f"d_patch{t}") for t in range(NT)]
        d_tok, d_rows, d_sel = sem("d_tok"), sem("d_rows"), sem("d_sel")
        d_id, d_qkv, d_rope, d_small, d_w0, d_l1 = (
            sem("d_id"), sem("d_qkv"), sem("d_rope"), sem("d_small"), sem("d_w0"), sem("d_l1"))
        d_w1, d_tail = sem("d_w1"), sem("d_tail")
        d_out = [sem("d_out0"), sem("d_out1")]
        s_setup = sem("s_setup")
        dve_setup = sem("dve_setup")
        s_lam = sem("s_lam")
        s_lame = sem("s_lame")
        s_v = sem("s_v")
        s_p = sem("s_p")
        proj_done, h_ready = sem("proj_done"), sem("h_ready")
        var_ready = [sem(f"var_ready{k}") for k in range(NORMS)]
        rstd_ready = [sem(f"rstd_ready{k}") for k in range(NORMS)]
        xn_ready = [sem(f"xn_ready{k}") for k in range(NORMS)]
        turned = [sem(f"turned{k}") for k in range(5)]
        copied = [sem(f"copied{k}") for k in range(5)]
        qkv_done, qkv_copied = sem("qkv_done"), sem("qkv_copied")
        rope_s_ready, rope_ready, prod1_ready = sem("rope_s_ready"), sem("rope_ready"), sem("prod1_ready")
        prodv_mine = sem("prodv_mine")
        s0_ready, p0_ready = sem("s0_ready"), sem("p0_ready")
        amix_ready, prodv_ready = sem("amix_ready"), sem("prodv_ready")
        att_ready, sq_ready, ms_ready, rms_ready = sem("att_ready"), sem("sq_ready"), sem("ms_ready"), sem("rms_ready")
        attn_ready = sem("attn_ready")
        wo_done, wo_added = sem("wo_done"), sem("wo_added")
        ffn_done, ffn_added = sem("ffn_done"), sem("ffn_added")
        wo1_done, wo1_added = sem("wo1_done"), sem("wo1_added")
        qk1_done, qk1_copied = sem("qk1_done"), sem("qk1_copied")
        x3_ready = sem("x3_ready")
        v1_done, v1_copied = sem("v1_done"), sem("v1_copied")
        s1_done, s1_sub, p1_ready = sem("s1_done"), sem("s1_sub"), sem("p1_ready")
        pt_done, pt_copied_a, pt_copied_v = sem("pt_done"), sem("pt_copied_a"), sem("pt_copied_v")
        pv_done, pv_copied, on_ready = sem("pv_done"), sem("pv_copied"), sem("on_ready")
        ot_done, ot_copied = sem("ot_done"), sem("ot_copied")
        logit_done, oh_ready, ohb_done = sem("logit_done"), sem("oh_ready"), sem("ohb_done")
        xm_ready, ohT_copied = sem("xm_ready"), sem("ohT_copied")
        ff_done, ff_ready, y_done = sem("ff_done"), sem("ff_ready"), sem("y_done")
        xbo_ready, hb_ready, yo_ready, y_taken = sem("xbo_ready"), sem("hb_ready"), sem("yo_ready"), sem("y_taken")

        def tile_cols(t):
            return slice(t * TT, (t + 1) * TT)

        def pair_cols(p, i):
            b = 2 * p + i
            at = (b // GB) * GN + (b % GB) * S
            return slice(at, at + S)

        block = ctx.enter_context(nc.Block())

        @block.sync
        def _(sp):
            sp.dma_start(tok_w_sb[:], tok_w).then_inc(d_tok, 16)
            sp.dma_start(patches_sb[:, 0], patches[:, 0]).then_inc(d_patch[0], 16)
            sp.dma_start(rows_sb[:], rows).then_inc(d_rows, 16)
            sp.dma_start(sel_sb[:], sel).then_inc(d_sel, 16)
            sp.dma_start(ident[:], ident_in).then_inc(d_id, 16)
            sp.dma_start(wqkv_sb[:], wqkv).then_inc(d_qkv, 16)
            sp.dma_start(rope_sb[0:TT], rope).then_inc(d_rope, 16)
            for dst, src in ((lam_sb, lam), (lnwb_sb, lnwb), (hmask_sb, hmask), (vmask_sb, vmask),
                             (causal_f, causal), (rowsel_f, rowsel), (disha_sb, disha)):
                sp.dma_start(dst[:], src).then_inc(d_small, 16)
            sp.dma_start(wo0_sb[:], wo0).then_inc(d_w0, 16)
            sp.dma_start(wf_sb[:], wf).then_inc(d_w0, 16)
            for t in range(1, NT):
                sp.dma_start(patches_sb[:, t], patches[:, t]).then_inc(d_patch[t], 16)
            for dst, src in ((wq1_sb, wq1), (wk1_sb, wk1), (wv1_sb, wv1), (wo1_sb, wo1), (vb, vones),
                             (wr_sb, wr), (b1_sb, b1)):
                sp.dma_start(dst[:], src).then_inc(d_l1, 16)
            sp.dma_start(w1_sb[:], w1).then_inc(d_w1, 16)
            sp.dma_start(wo2_sb[:], wo2).then_inc(d_w1, 16)
            sp.dma_start(tail_sb[:], tail).then_inc(d_tail, 16)
            for t in range(NT):
                sp.wait_ge(yo_ready, t + 1)
                sp.dma_start(out[tile_cols(t), :], yo[0:TT, t % 2, :]).then_inc(d_out[t % 2], 16)
            sp.wait_ge(d_out[0], 16 * (NT // 2))
            sp.wait_ge(d_out[1], 16 * (NT // 2))

        @block.tensor
        def _(pe):
            mm = nc.tensor.matmul

            def turn(k, t, src, psum, rows_=TT):
                for c in range(EC):
                    last = nc.tensor.transpose(psum[:, c * P:c * P + rows_], src[0:rows_, c * P:(c + 1) * P],
                                               ident[0:rows_, 0:rows_])
                last.then_inc(turned[k], 1)

            def project(t):
                pe.wait_ge(d_patch[t], 16)
                if t:
                    pe.wait_ge(h_ready, t)
                for c in range(PC):
                    mm(bank[2][0:TT, 0:E], patches_sb[:, t, c, :], tok_w_sb[:, c, :],
                       start=(c == 0), stop=False)
                mm(bank[2][0:TT, 0:E], sel_sb[:, tile_cols(t)], rows_sb[:, :],
                   start=False, stop=True).then_inc(proj_done, 1)

            def to_qkv(t):
                pe.wait_ge(xn_ready[0], t + 1)
                if t:
                    pe.wait_ge(copied[0], t)
                turn(0, t, xn[:, t, :], bank[4])
                pe.wait_ge(copied[0], t + 1)
                if t:
                    pe.wait_ge(qkv_copied, 2 * t)
                for c in range(EC):
                    mm(bank[0][0:TT, :], xT0[:, c, :], wqkv_sb[:, c, 0:2 * E], start=(c == 0), stop=(c == EC - 1))
                for c in range(EC):
                    last = mm(bank[1][0:TT, 0:E], xT0[:, c, :], wqkv_sb[:, c, 2 * E:3 * E],
                              start=(c == 0), stop=(c == EC - 1))
                last.then_inc(qkv_done, 1)

            def to_wo(t):
                pe.wait_ge(attn_ready, t + 1)
                if t:
                    pe.wait_ge(copied[2], t)
                turn(1, t, attn_n, bank[5])
                pe.wait_ge(copied[1], t + 1)
                if t:
                    pe.wait_ge(ffn_added, t)
                else:
                    pe.wait_ge(d_w0, 32)
                    pe.wait_ge(s_setup, 1)
                for c in range(EC):
                    last = mm(bank[3][0:TT, 0:E], aT[:, c, :], wo0_sb[:, c, :], start=(c == 0), stop=(c == EC - 1))
                last.then_inc(wo_done, 1)

            def to_ffn(t):
                pe.wait_ge(xn_ready[1], t + 1)
                turn(2, t, xn[:, t, :], bank[5])
                pe.wait_ge(copied[2], t + 1)
                pe.wait_ge(wo_added, t + 1)
                for c in range(EC):
                    last = mm(bank[3][0:TT, 0:E], xTf[:, c, :], wf_sb[:, c, :], start=(c == 0), stop=(c == EC - 1))
                last.then_inc(ffn_done, 1)

            def to_second(t):
                pe.wait_ge(xn_ready[2], t + 1)
                if t:
                    pe.wait_ge(copied[3], t)
                turn(3, t, xn[:, t, :], bank[6])

            def qk_unit(g, i, o):
                w, c_out = (wq1_sb, i) if i < EC else (wk1_sb, i - EC)
                if g or i:
                    pe.wait_ge(qk1_copied, 2 * EC * g + i)
                else:
                    pe.wait_ge(d_l1, 16 * 7)
                if i == 0:
                    pe.wait_ge(copied[3], GT * (g + 1))
                for c in range(EC):
                    last = mm(o[:, 0:GN], w[:, c, c_out * P:(c_out + 1) * P],
                              x1T[:, c, g * GN:(g + 1) * GN], start=(c == 0), stop=(c == EC - 1))
                last.then_inc(qk1_done, 1)

            for s_, n in ((d_tok, 16), (d_rows, 16), (d_sel, 16)):
                pe.wait_ge(s_, n)
            project(0)
            project(1)
            pe.wait_ge(d_id, 16)
            pe.wait_ge(d_qkv, 16)
            for t in range(-1, NT + 2):
                if 1 <= t <= NT:
                    to_wo(t - 1)
                if t >= 2:
                    to_second(t - 2)
                if t + 1 < NT:
                    to_qkv(t + 1)
                if 2 <= t + 2 < NT:
                    project(t + 2)
                if 1 <= t <= NT:
                    to_ffn(t - 1)
                for i in QK_EARLY.get(t, ()):
                    qk_unit(0, i, bank[7])

            def values(p):
                pe.wait_ge(x3_ready, p + 1)
                if p:
                    pe.wait_ge(v1_copied, p)
                for i in range(2):
                    for c in range(EC):
                        last = mm(bank[7][0:KR, i * E:(i + 1) * E],
                                  x3[:, p % 2, i, c, :, :].rearrange("p j k -> p (j k)"), wv1_sb[:, c, :],
                                  start=(c == 0), stop=(c == EC - 1))
                last.then_inc(v1_done, 1)

            def scores(p):
                g = 2 * p // GB
                pe.wait_ge(qk1_copied, 2 * EC * (g + 1))
                if p:
                    pe.wait_ge(s1_sub, p)
                for c in range(EC):
                    o = bank[c][:, 0:HC * S]
                    mm(o, rowsel_sb[:, :], causal_sb[:, :].unsqueeze(1).to_broadcast([S, HC, S]),
                       start=True, stop=False, skip_group_check=True)
                    for i in range(2):
                        b = (2 * p + i) % GB
                        last = mm(bank[c][HALF * i:HALF * i + S, 0:HC * S], qT[:, g, c, b * S:(b + 1) * S],
                                  km[g][:, c, b, :, :], start=False, stop=(i == 1), skip_group_check=True)
                last.then_inc(s1_done, 1)

            def turn_probs(p):
                pe.wait_ge(p1_ready, p + 1)
                if p:
                    pe.wait_ge(pv_copied, p)
                pf = prob[:, p % 2, :, :, :].rearrange("p c h k -> p (c h k)")
                for c in range(KC):
                    r = KR if c < KC - 1 else S
                    last = nc.tensor.transpose(bank[2 + c // 4][0:r, (c % 4) * P:(c % 4 + 1) * P],
                                               pf[:, c * KR:c * KR + r], ident[:, :])
                last.then_inc(pt_done, 1)

            def mix_values(p):
                pe.wait_ge(pt_copied_a, p + 1)
                pe.wait_ge(pt_copied_v, p + 1)
                pe.wait_ge(v1_copied, p + 1)
                for c in range(KC):
                    r, w = (KR, KT * VW) if c < KC - 1 else (S, VW)
                    at = (c % 4) * 2 * KT * VW
                    o = bank[2 + c // 4][0:HALF + S, at:at + 2 * KT * VW].rearrange("p (i w) -> p i w", i=2)
                    last = mm(o[:, :, 0:w], pT[0:r, p % 2, c, 0:HALF + S],
                              vb[0:r, p % 2, c, :, :, :].rearrange("p i j w -> p i (j w)")[:, :, 0:w],
                              start=True, stop=True)
                last.then_inc(pv_done, 1)

            def turn_mixed(p):
                pe.wait_ge(on_ready, p + 1)
                if p:
                    pe.wait_ge(ot_copied, p)
                for c in range(EC):
                    last = nc.tensor.transpose(bank[4][:, c * P:(c + 1) * P], on[:, p % 2, c * P:(c + 1) * P],
                                               ident[:, :])
                last.then_inc(ot_done, 1)

            def route(t, step_):
                if step_ == 0:
                    if t % GT == 0:
                        pe.wait_ge(ot_copied, (t // GT + 1) * PAIRS // G)
                        pe.wait_ge(qk1_copied, 2 * EC * G)
                    if t:
                        pe.wait_ge(copied[4], t)
                    for c in range(EC):
                        last = mm(bank[5][0:TT, 0:E], aT1[:, c, tile_cols(t)], wo1_sb[:, c, :],
                                  start=(c == 0), stop=(c == EC - 1))
                    last.then_inc(wo1_done, 1)
                elif step_ == 1:
                    pe.wait_ge(xn_ready[3], t + 1)
                    turn(4, t, xn[:, t, :], bank[5])
                elif step_ == 2:
                    pe.wait_ge(copied[4], t + 1)
                    if t:
                        pe.wait_ge(xm_ready, t)
                        pe.wait_ge(ohT_copied, t)
                    for c in range(EC):
                        last = mm(bank[6][0:TT, 0:NX], x3T[:, c, tile_cols(t)], wr_sb[:, c, :],
                                  start=(c == 0), stop=(c == EC - 1))
                    last.then_inc(logit_done, 1)
                else:
                    pe.wait_ge(oh_ready, t + 1)
                    for e in range(NX):
                        mm(bank[6][:, e * TT:(e + 1) * TT], oh[0:TT, t % 2, e:e + 1].to_broadcast([TT, P]),
                           identb[0:TT, 0:TT], start=True, stop=True)
                    mm(bank[6][0:NX, NX * TT:NX * TT + TT], oh[0:TT, t % 2, :], identb[0:TT, 0:TT],
                       start=True, stop=True).then_inc(ohb_done, 1)

            scores(0)
            values(0)
            for p in range(PAIRS):
                if p + 1 < PAIRS:
                    scores(p + 1)
                    values(p + 1)
                turn_probs(p)
                for i in QK_LATE.get(p, ()):
                    qk_unit(1, i, bank[5 + i % 2])
                if p:
                    turn_mixed(p - 1)
                if p >= PAIRS // G:
                    for i, step_ in route_steps(2 * (p - PAIRS // G)):
                        route(i, step_)
                mix_values(p)
                if p >= PAIRS // G:
                    for i, step_ in route_steps(2 * (p - PAIRS // G) + 1):
                        route(i, step_)
            turn_mixed(PAIRS - 1)

            pe.wait_ge(d_w1, 32)

            def experts(g, f):
                n = g * FC + f
                cols = slice(g * GN, (g + 1) * GN)
                if f == 0:
                    pe.wait_ge(xm_ready, GT * (g + 1))
                    pe.wait_ge(ohT_copied, GT * (g + 1))
                if n >= 2:
                    pe.wait_ge(ff_ready, n - 1)
                o = bank[n % 2][:, 0:GN]
                for e in range(NX):
                    for c in range(EC):
                        mm(o, w1_sb[:, c, e, f * P:(f + 1) * P], xm[:, c, e, cols],
                           start=(e == 0 and c == 0), stop=False)
                mm(o, b1_sb[:, f * P:(f + 1) * P], ohT[:, cols], start=False, stop=True).then_inc(ff_done, 1)

            def down(t):
                pe.wait_ge(ff_ready, FC * (t // GT + 1))
                if t >= 2:
                    pe.wait_ge(y_taken, t - 1)
                for f in range(FC):
                    last = mm(bank[2 + t % 2][0:TT, 0:E], hT[:, f, tile_cols(t)], wo2_sb[:, f, :],
                              start=(f == 0), stop=(f == FC - 1))
                last.then_inc(y_done, 1)

            for f in range(FC):
                experts(0, f)
                for i, step_ in route_steps(f):
                    route(GT + i, step_)
            for f in range(FC):
                experts(1, f)
                if f % 2 and f // 2 < GT:
                    down(f // 2)
            for t in range(GT, NT):
                down(t)

        @block.scalar
        def _(act):
            fn = nc.scalar.activation

            def turn_out(k, t, psum, dst, **affine):
                act.wait_ge(turned[k], t + 1)
                fn(dst, psum[:, 0:EC * P].rearrange("p (c n) -> p c n", c=EC)[:, :, 0:TT],
                   ACT.Identity if affine else ACT.Copy, **affine).then_inc(copied[k], 1)

            def h_copy(t):
                act.wait_ge(proj_done, t + 1)
                fn(h[0:TT, t, :], bank[2][0:TT, 0:E], ACT.Copy).then_inc(h_ready, 1)

            def qkv_out(t):
                act.wait_ge(qkv_done, t + 1)
                if t >= 1:
                    act.wait_ge(rope_ready, t)
                if t >= 2:
                    act.wait_ge(prodv_ready, t - 1)
                    act.wait_ge(att_ready, t - 1)
                fn(qk[0:TT, :], bank[0][0:TT, :], ACT.Copy).then_inc(qkv_copied, 1)
                fn(v0[0:TT, t % 2, :], bank[1][0:TT, 0:E], ACT.Copy).then_inc(qkv_copied, 1)

            def exps(t):
                act.wait_ge(s0_ready, t + 1)
                fn(s0[0:TT], s0[0:TT], ACT.Exp, scale=SCALE0).then_inc(p0_ready, 1)

            def squares(t):
                act.wait_ge(att_ready, t + 1)
                fn(attsq[0:TT, :], att[0:TT, :], ACT.Square).then_inc(sq_ready, 1)

            def qk_unit(g, i, psum):
                act.wait_ge(qk1_done, 2 * EC * g + i + 1)
                if i < EC:
                    fn(qT[:, g, i, :], psum[:, 0:GN], ACT.Copy).then_inc(qk1_copied, 1)
                    return
                src = psum[:, 0:GB * S].rearrange("p (b k) -> p b k", b=GB)
                for j in range(HC):
                    last = fn(km[g][:, i - EC, :, j, :], src, ACT.Copy, scale=hmask_sb[:, j:j + 1])
                last.then_inc(qk1_copied, 1)

            h_copy(0)
            h_copy(1)
            for t in range(-1, NT + 2):
                if 1 <= t <= NT:
                    if t == 1:
                        act.wait_ge(dve_setup, 1)
                    turn_out(1, t - 1, bank[5], aT[:, :, :], scale=lnwb_s[:, 0:1], bias=lnwb_s[:, 1:2])
                if 0 <= t < NT:
                    exps(t)
                if t >= 2:
                    turn_out(3, t - 2, bank[6], x1T[:, :, tile_cols(t - 2)])
                if t + 1 < NT:
                    turn_out(0, t + 1, bank[4], xT0[:, :, :])
                    qkv_out(t + 1)
                if t == -1:
                    act.wait_ge(s_lam, 1)
                    fn(lam_e[:, :], lam_e[:, :], ACT.Exp).then_inc(s_lame, 1)
                if 0 <= t < NT:
                    squares(t)
                if 2 <= t + 2 < NT:
                    h_copy(t + 2)
                if 1 <= t <= NT:
                    turn_out(2, t - 1, bank[5], xTf[:, :, :])
                for i in QK_EARLY.get(t, ()):
                    qk_unit(0, i, bank[7])

            def probs(p):
                act.wait_ge(s1_sub, p + 1)
                x = prob[:, p % 2, :, :, :]
                fn(x, x, ACT.Exp, scale=SCALE1).then_inc(p1_ready, 1)

            def probs_out(p):
                act.wait_ge(pt_done, p + 1)
                if p >= 2:
                    act.wait_ge(pv_done, p - 1)
                fn(pT[:, p % 2, 0:4, :], bank[2][0:KR, :].rearrange("p (c n) -> p c n", c=4),
                   ACT.Copy).then_inc(pt_copied_a, 1)

            def mixed_out(p):
                act.wait_ge(pv_done, p + 1)
                if p >= 2:
                    act.wait_ge(on_ready, p - 1)
                for i in range(2):
                    rows_ = slice(HALF * i, HALF * i + S)
                    o = bank[2][rows_, 0:8 * KT * VW].rearrange("p (c i w) -> p c i w", c=4, i=2)
                    fn(oc[rows_, p % 2, 0:4 * KT, :].rearrange("p (c j) w -> p c (j w)", c=4), o[:, :, i, :], ACT.Copy)
                    at = i * KT * VW
                    fn(oc[rows_, p % 2, 4 * KT:5 * KT, :].rearrange("p j w -> p (j w)"),
                       bank[3][rows_, at:at + KT * VW], ACT.Copy)
                    at += 2 * KT * VW
                    last = fn(oc[rows_, p % 2, 5 * KT, :], bank[3][rows_, at:at + VW], ACT.Copy)
                last.then_inc(pv_copied, 1)

            def mixed_turned(p):
                act.wait_ge(ot_done, p + 1)
                at = pair_cols(p, 0).start
                fn(aT1[:, :, at:at + 2 * S].rearrange("p c (i n) -> p c i n", i=2),
                   bank[4][:, 0:EC * P].rearrange("p (c i n) -> p c i n", c=EC, i=2)[:, :, :, 0:S],
                   ACT.Copy).then_inc(ot_copied, 1)

            def route(t, step_):
                if step_ == 1:
                    turn_out(4, t, bank[5], x3T[:, :, tile_cols(t)])
                elif step_ == 3:
                    act.wait_ge(xm_ready, t + 1)
                    fn(ohT[:, tile_cols(t)], bank[6][0:NX, NX * TT:NX * TT + TT], ACT.Copy).then_inc(ohT_copied, 1)

            probs(0)
            for p in range(PAIRS):
                if p + 1 < PAIRS:
                    probs(p + 1)
                probs_out(p)
                for i in QK_LATE.get(p, ()):
                    qk_unit(1, i, bank[5 + i % 2])
                if p:
                    mixed_turned(p - 1)
                if p >= PAIRS // G:
                    for i, step_ in route_steps(2 * (p - PAIRS // G)):
                        route(i, step_)
                mixed_out(p)
                if p >= PAIRS // G:
                    for i, step_ in route_steps(2 * (p - PAIRS // G) + 1):
                        route(i, step_)
            mixed_turned(PAIRS - 1)

            def experts(g, f):
                n = g * FC + f
                act.wait_ge(ff_done, n + 1)
                fn(hT[:, f, g * GN:(g + 1) * GN], bank[n % 2][:, 0:GN], ACT.Gelu).then_inc(ff_ready, 1)

            for f in range(FC):
                experts(0, f)
                for i, step_ in route_steps(f):
                    route(GT + i, step_)
            for f in range(FC):
                experts(1, f)

        @block.vector
        def _(dve):
            tt, ts, red = nc.vector.tensor_tensor, nc.vector.tensor_scalar, nc.vector.tensor_reduce
            count = [0]
            r = slice(0, TT)

            def mark(ins):
                count[0] += 1
                ins.then_inc(s_v, 1)
                return count[0]

            def need(n):
                dve.wait_ge(s_v, n)

            def step(ins):
                need(mark(ins))

            def moments_1(k, t, src):
                return mark(nc.vector.bn_stats(stats[r, k, t, :], src))

            def moments_2(k, t, n):
                need(n)
                return mark(nc.vector.bn_aggr(mean[r, k, t, :], stats[r, k, t, :]))

            def moments_3(k, t, n, eps):
                need(n)
                ts(vare[r, k, t, :], mean[r, k, t, 1:2], eps, None, ALU.add).then_inc(var_ready[k], 1)

            def moments(k, t, src, eps):
                moments_3(k, t, moments_2(k, t, moments_1(k, t, src)), eps)

            def normed(k, t, src, dst):
                dve.wait_ge(rstd_ready[k], t + 1)
                ts(dst, src, mean[r, k, t, 0:1], rstd[r, k, t, :], ALU.subtract, ALU.mult).then_inc(xn_ready[k], 1)

            def prepare():
                dve.wait_ge(d_small, 16 * 7)
                step(tt(lam_p[:], lam_sb[:, :, 0, :], lam_sb[:, :, 1, :], ALU.mult))
                red(lam_e[:, :], lam_p[:], AX, ALU.add).then_inc(s_lam, 1)
                step(ts(lnwb_s[:, :], lnwb_sb[:, :], 1.0 - LAMBDA_INIT, None, ALU.mult))
                dve.wait_ge(s_lame, 1)
                step(tt(neg_lam[:], lam_e[:, 1:2], lam_e[:, 0:1], ALU.subtract))
                step(ts(neg_lam[:], neg_lam[:], -LAMBDA_INIT, None, ALU.add))
                nc.vector.memset(oc[:], 1.0).then_inc(dve_setup, 1)

            def halves(x):
                return x.rearrange("p (n a d) -> p n a d", n=H0, a=2)

            q, k_ = halves(qk_c[r, 0:E]), halves(qk_c[r, E:2 * E])
            av = att[r, :].rearrange("p (n e) -> p n e", n=H0)
            mx, sm, rc = (small[r, i] for i in range(3))

            def added(k, t, done, psum, gone):
                dve.wait_ge(done, t + 1)
                tt(h[r, t, :], h[r, t, :], psum[r, 0:E], ALU.add).then_inc(gone, 1)
                dve.wait_ge(gone, t + 1)
                moments(k, t, h[r, t, :], LN_EPS)

            def attend(t):
                here, before, after = 0 <= t < NT, 1 <= t <= NT, t + 1 < NT
                if here:
                    step(tt(prod[r, 0], q[:, :, 0, :].unsqueeze(2).to_broadcast([TT, H0, H0, D0]),
                            k_[:, :, 0, :].unsqueeze(1).to_broadcast([TT, H0, H0, D0]), ALU.mult))
                    summed = mark(red(s0[r, 0], prod[r, 0], AX, ALU.add))
                if t >= 2:
                    dve.wait_ge(ffn_done, t - 1)
                    tt(h[r, t - 2, :], h[r, t - 2, :], bank[3][r, 0:E], ALU.add).then_inc(ffn_added, 1)
                if before:
                    dve.wait_ge(rms_ready, t)
                    tt(attn_n[r, :].rearrange("p (n e) -> p n e", n=H0), av,
                       ms[r, (t - 1) % 2, 1, :].unsqueeze(2).to_broadcast([TT, H0, 2 * D0]),
                       ALU.mult).then_inc(attn_ready, 1)
                if after:
                    dve.wait_ge(h_ready, t + 2)
                    m = moments_1(0, t + 1, h[r, t + 1, :])
                if t >= 2:
                    dve.wait_ge(ffn_added, t - 1)
                    m2 = moments_1(2, t - 2, h[r, t - 2, :])
                if here:
                    dve.wait_ge(prod1_ready, t + 1)
                    second = mark(red(s0[r, 1], prod[r, 1], AX, ALU.add))
                if after:
                    m = moments_2(0, t + 1, m)
                if t >= 2:
                    m2 = moments_2(2, t - 2, m2)
                if here:
                    need(summed)
                    need(second)
                    top = mark(red(mx, s0[r], AX, ALU.max))
                if after:
                    moments_3(0, t + 1, m, LN_EPS)
                if t >= 2:
                    moments_3(2, t - 2, m2, LN_EPS)
                if here:
                    need(top)
                    tt(s0[r], s0[r], mx.unsqueeze(3).to_broadcast([TT, 2, H0, H0]), ALU.subtract).then_inc(s0_ready, 1)
                if after:
                    normed(0, t + 1, h[r, t + 1, :], xn[r, t + 1, :])
                if t >= 2:
                    normed(2, t - 2, h[r, t - 2, :], xn[r, t - 2, :])
                if here:
                    dve.wait_ge(p0_ready, t + 1)
                    step(red(sm, s0[r], AX, ALU.add))
                    step(nc.vector.reciprocal(rc, sm))
                    step(ts(rc[:, 1, :], rc[:, 1, :], neg_lam[r, :], None, ALU.mult))
                    step(tt(s0[r], s0[r], rc.unsqueeze(3).to_broadcast([TT, 2, H0, H0]), ALU.mult))
                    tt(amix[r], s0[r, 0], s0[r, 1], ALU.add).then_inc(amix_ready, 1)
                    dve.wait_ge(amix_ready, t + 1)
                    if before:
                        dve.wait_ge(attn_ready, t)
                    tt(prodv[r, 0:NV], amix[r, 0:NV].unsqueeze(2).to_broadcast([TT, NV, 2 * D0, H0]),
                       v0[r, t % 2, :].rearrange("p (m e) -> p e m", m=H0).unsqueeze(1)
                       .to_broadcast([TT, NV, 2 * D0, H0]), ALU.mult).then_inc(prodv_mine, 1)
                if before:
                    dve.wait_ge(wo_done, t)
                    tt(h[r, t - 1, :], h[r, t - 1, :], bank[3][r, 0:E], ALU.add).then_inc(wo_added, 1)
                if here:
                    dve.wait_ge(prodv_mine, t + 1)
                    red(av[:, 0:NV, :], prodv[r, 0:NV], AX, ALU.add)
                if before:
                    dve.wait_ge(wo_added, t)
                    moments(1, t - 1, h[r, t - 1, :], LN_EPS)
                if here:
                    dve.wait_ge(prodv_ready, t + 1)
                    red(av[:, NV:H0, :], prodv[r, NV:H0], AX, ALU.add).then_inc(att_ready, 1)
                if before:
                    normed(1, t - 1, h[r, t - 1, :], xn[r, t - 1, :])
                if after:
                    dve.wait_ge(qkv_copied, 2 * t + 4)
                    cos = rope_sb[r, t + 1, 0, :].unsqueeze(1).to_broadcast([TT, 4 * H0, D0])
                    turned_c = mark(tt(qk_c[r, :].rearrange("p (g d) -> p g d", d=D0),
                                       qk[r, :].rearrange("p (g d) -> p g d", d=D0), cos, ALU.mult))
                if here:
                    dve.wait_ge(sq_ready, t + 1)
                    step(red(ms[r, t % 2, 0, :], attsq[r, :].rearrange("p (n e) -> p n e", n=H0), AX, ALU.add))
                    ts(ms[r, t % 2, 0, :], ms[r, t % 2, 0, :], 1.0 / (2 * D0), RMS_EPS,
                       ALU.mult, ALU.add).then_inc(ms_ready, 1)
                if after:
                    need(turned_c)
                    dve.wait_ge(rope_s_ready, t + 2)
                    tt(qk_c[r, :], qk_c[r, :], qk_s[r, :], ALU.add).then_inc(rope_ready, 1)
                if after:
                    dve.wait_ge(rope_ready, t + 2)

            dve.wait_ge(d_rope, 16)
            attend(-1)
            prepare()
            for t in range(NT + 2):
                attend(t)

            dve.wait_ge(d_l1, 16 * 7)

            def softmax_in(p):
                dve.wait_ge(s1_done, p + 1)
                if p >= 2:
                    dve.wait_ge(pt_done, p - 1)
                for c in range(EC):
                    sc = bank[c][:, 0:HC * S].rearrange("p (h k) -> p h k", h=HC)
                    m = smx[:, p % 2, c, :]
                    step(red(m, sc, AX, ALU.max))
                    last = tt(prob[:, p % 2, c], sc, m.unsqueeze(2).to_broadcast([P, HC, S]), ALU.subtract)
                last.then_inc(s1_sub, 1)

            def values(p):
                dve.wait_ge(v1_done, p + 1)
                if p >= 2:
                    dve.wait_ge(pv_done, p - 1)
                nf = KC - 1
                for i in range(2):
                    src = bank[7][0:KR, i * E:i * E + nf * KT * D1].rearrange("p (c j e) -> p c j e", c=nf, j=KT)
                    tt(vb[:, p % 2, 0:nf, i, :, 0:D1], src, vmask_sb[:, :, :].unsqueeze(1).to_broadcast([KR, nf, KT, D1]),
                       ALU.mult)
                    last = nc.vector.tensor_copy(vb[0:S, p % 2, nf, i, 0, 0:D1],
                                                 bank[7][0:S, i * E + nf * KT * D1:(i + 1) * E])
                last.then_inc(v1_copied, 1)

            def probs_out(p):
                dve.wait_ge(pt_done, p + 1)
                nc.vector.tensor_copy(pT[:, p % 2, 4, :], bank[3][0:KR, 0:P])
                nc.vector.tensor_copy(pT[0:S, p % 2, 5, :], bank[3][0:S, P:2 * P]).then_inc(pt_copied_v, 1)

            def mixed(p):
                dve.wait_ge(pv_copied, p + 1)
                if p >= 2:
                    dve.wait_ge(ot_done, p - 1)
                if p:
                    dve.wait_ge(on_ready, p)
                step(nc.vector.reciprocal(orc[:, :], oc[:, p % 2, :, D1]))
                tt(on[:, p % 2, :].rearrange("p (h e) -> p h e", h=H1), oc[:, p % 2, :, 0:D1],
                   orc[:, :].unsqueeze(2).to_broadcast([P, H1, D1]), ALU.mult).then_inc(on_ready, 1)

            def route(t, step_):
                if step_ == 0:
                    added(3, t, wo1_done, bank[5], wo1_added)
                elif step_ == 1:
                    normed(3, t, h[r, t, :], xn[r, t, :])
                elif step_ == 2:
                    dve.wait_ge(logit_done, t + 1)
                    step(red(lmax[r, :], bank[6][r, 0:NX], AX, ALU.max))
                    step(nc.vector.scalar_tensor_tensor(out=lcand[r, :], in0=bank[6][r, 0:NX], scalar=lmax[r, :],
                                                        in1=tie_sb[r, :], op0=ALU.is_equal, op1=ALU.mult))
                    step(red(lmax[r, :], lcand[r, :], AX, ALU.max))
                    ts(oh[r, t % 2, :], lcand[r, :], lmax[r, :], None, ALU.is_equal).then_inc(oh_ready, 1)
                    dve.wait_ge(oh_ready, t + 1)
                else:
                    dve.wait_ge(ohb_done, t + 1)
                    for c in range(EC):
                        last = tt(xm[:, c, :, tile_cols(t)],
                                  bank[6][:, 0:NX * TT].rearrange("p (x n) -> p x n", x=NX),
                                  x3T[:, c, tile_cols(t)].unsqueeze(1).to_broadcast([P, NX, TT]), ALU.mult)
                    last.then_inc(xm_ready, 1)

            softmax_in(0)
            values(0)
            for p in range(PAIRS):
                if p + 1 < PAIRS:
                    softmax_in(p + 1)
                    values(p + 1)
                if p == PAIRS // G:
                    dve.wait_ge(d_tail, 16)
                probs_out(p)
                if p >= PAIRS // G:
                    for i, step_ in route_steps(2 * (p - PAIRS // G)):
                        route(i, step_)
                mixed(p)
                if p >= PAIRS // G:
                    for i, step_ in route_steps(2 * (p - PAIRS // G) + 1):
                        route(i, step_)

            def finish(t):
                dve.wait_ge(y_done, t + 1)
                dve.wait_ge(xbo_ready, t + 1)
                tt(y[r, t % 2, :], bank[2 + t % 2][r, 0:E], xbo[r, t % 2, :], ALU.add).then_inc(y_taken, 1)
                dve.wait_ge(y_taken, t + 1)
                moments(4, t, y[r, t % 2, :], LN_EPS_OUT)
                normed(4, t, y[r, t % 2, :], y[r, t % 2, :])
                dve.wait_ge(xn_ready[4], t + 1)
                step(tt(y[r, t % 2, :], y[r, t % 2, :], gamma_sb[r, :], ALU.mult))
                dve.wait_ge(hb_ready, t + 1)
                if t >= 2:
                    dve.wait_ge(d_out[t % 2], 16 * (t // 2))
                tt(yo[r, t % 2, :], y[r, t % 2, :], hb[r, t % 2, :], ALU.add).then_inc(yo_ready, 1)
                dve.wait_ge(yo_ready, t + 1)

            for f in range(FC):
                for i, step_ in route_steps(f):
                    route(GT + i, step_)
            for t in range(NT):
                finish(t)

        @block.gpsimd
        def _(pool):
            tt = nc.gpsimd.tensor_tensor
            r = slice(0, TT)
            nc.gpsimd.memset(expo[:, :], -0.5).then_inc(s_p, 1)
            for g in range(G):
                nc.gpsimd.memset(aT1[:, :, g * GN + GB * S:(g + 1) * GN], 0.0)
            pool.wait_ge(d_id, 16)
            nc.gpsimd.tensor_copy(identb[:, :], ident[:, :])
            pool.wait_ge(d_small, 16 * 7)
            nc.gpsimd.tensor_copy(causal_sb[:, :], causal_f[:, :])
            nc.gpsimd.tensor_copy(rowsel_sb[:, :], rowsel_f[:, :])
            pool.wait_ge(d_w0, 32)
            tt(wf_sb[:], wf_sb[:], disha_sb[:, :].unsqueeze(1).to_broadcast([P, EC, E]), ALU.add).then_inc(s_setup, 1)
            pool.wait_ge(s_p, 1)

            def power(k, t):
                pool.wait_ge(var_ready[k], t + 1)
                tt(rstd[r, k, t, :], vare[r, k, t, :], expo[r, 0:1], ALU.pow).then_inc(rstd_ready[k], 1)

            q = qk_c[r, 0:E].rearrange("p (n a d) -> p n a d", n=H0, a=2)
            k_ = qk_c[r, E:2 * E].rearrange("p (n a d) -> p n a d", n=H0, a=2)

            def products(t):
                pool.wait_ge(rope_ready, t + 1)
                tt(prod[r, 1], q[:, :, 1, :].unsqueeze(2).to_broadcast([TT, H0, H0, D0]),
                   k_[:, :, 1, :].unsqueeze(1).to_broadcast([TT, H0, H0, D0]), ALU.mult).then_inc(prod1_ready, 1)

            def value_products(t):
                pool.wait_ge(amix_ready, t + 1)
                nv = H0 - NV
                tt(prodv[r, NV:H0], amix[r, NV:H0].unsqueeze(2).to_broadcast([TT, nv, 2 * D0, H0]),
                   v0[r, t % 2, :].rearrange("p (m e) -> p e m", m=H0).unsqueeze(1).to_broadcast([TT, nv, 2 * D0, H0]),
                   ALU.mult).then_inc(prodv_ready, 1)

            def rotary(t):
                pool.wait_ge(qkv_copied, 2 * t + 1)
                if t == 0:
                    pool.wait_ge(d_rope, 16)
                else:
                    pool.wait_ge(rope_ready, t)
                half = D0 // 2
                x = qk[r, :].rearrange("p (g a d) -> p g a d", a=2, d=half)
                xs = qk_s[r, :].rearrange("p (g a d) -> p g a d", a=2, d=half)
                for a in range(2):
                    sin = rope_sb[r, t, 1, a * half:(a + 1) * half].unsqueeze(1).to_broadcast([TT, 4 * H0, half])
                    last = tt(xs[:, :, a, :], x[:, :, 1 - a, :], sin, ALU.mult)
                last.then_inc(rope_s_ready, 1)

            def rms_power(t):
                pool.wait_ge(ms_ready, t + 1)
                tt(ms[r, t % 2, 1, :], ms[r, t % 2, 0, :], expo[r, 0:H0], ALU.pow).then_inc(rms_ready, 1)

            for t in range(-1, NT + 2):
                here, before, after = 0 <= t < NT, 1 <= t <= NT, t + 1 < NT
                if here:
                    products(t)
                if after:
                    power(0, t + 1)
                if t >= 2:
                    power(2, t - 2)
                if here:
                    value_products(t)
                if before:
                    power(1, t - 1)
                if after:
                    rotary(t + 1)
                if here:
                    rms_power(t)

            def repeat(p):
                pool.wait_ge(copied[3], NT)
                if p >= 2:
                    pool.wait_ge(v1_done, p - 1)
                for i in range(2):
                    for c in range(EC):
                        last = nc.gpsimd.tensor_copy(
                            x3[:, p % 2, i, c],
                            x1T[:, c, pair_cols(p, i)].unsqueeze(1).to_broadcast([P, KT, S]))
                last.then_inc(x3_ready, 1)

            repeat(0)
            for p in range(PAIRS):
                if p + 1 < PAIRS:
                    repeat(p + 1)
                if p >= PAIRS // G:
                    for slot in range(2 * (p - PAIRS // G), 2 * (p - PAIRS // G) + 2):
                        for i, step_ in route_steps(slot):
                            if step_ == 0:
                                power(3, i)

            pool.wait_ge(d_tail, 16)

            def residual(t):
                pool.wait_ge(xn_ready[3], t + 1)
                if t >= 2:
                    pool.wait_ge(yo_ready, t - 1)
                tt(xbo[r, t % 2, :], xn[r, t, :], bo_sb[r, :], ALU.add).then_inc(xbo_ready, 1)
                tt(hb[r, t % 2, :], h[r, t, :], beta_sb[r, :], ALU.add).then_inc(hb_ready, 1)

            for t in range(GT, NT):
                power(3, t)
            residual(0)
            residual(1)
            for t in range(NT):
                power(4, t)
                if t + 2 < NT:
                    residual(t + 2)


def rope_tables():
    inv = (1.0 / np.float32(10000.0) ** (np.arange(0, D0, 2, dtype=np.float32) / np.float32(D0))).astype(np.float32)
    slot = np.arange(N) % GN
    pos = (slot % S).astype(np.float32)
    f = pos[:, None] * inv[None, :]
    cos, sin = np.cos(f), np.sin(f)
    t = np.stack([np.concatenate([cos, cos], 1), np.concatenate([-sin, sin], 1)], 1).astype(np.float32)
    return np.ascontiguousarray(t.reshape(NT, TT, 2, D0).transpose(1, 0, 2, 3))


def kernel(x, cls_tok, L0_tok_W, L0_tok_b, L0_tok_cls_token, L0_tok_pos_embed, L0_attn_Wq, L0_attn_Wk,
           L0_attn_Wv, L0_attn_Wo, L0_attn_lambda_q1, L0_attn_lambda_k1, L0_attn_lambda_q2,
           L0_attn_lambda_k2, L0_attn_ln_w, L0_attn_ln_b, L0_ffn_weight, L0_ffn_disha, L1_attn_q_proj,
           L1_attn_k_proj, L1_attn_v_proj, L1_attn_o_proj, L1_ffn_W_router, L1_ffn_W1, L1_ffn_b1,
           L1_ffn_Wo, L1_ffn_bo, L1_ffn_ln_gamma, L1_ffn_ln_beta):
    from concourse import bacc
    from concourse.bass_utils import run_bass_kernel_spmd

    a = np.asarray

    def chunks(w):
        w = a(w)
        return np.ascontiguousarray(w.reshape(w.shape[0] // P, P, w.shape[1]).transpose(1, 0, 2))

    def tiled(v, reps):
        return np.concatenate([a(v)] * reps, axis=0)

    pt = a(x).reshape(B, CIN, NP, PATCH, NP, PATCH).transpose(0, 2, 4, 1, 3, 5).reshape(B, NP * NP, PD)
    slots = np.zeros((G, GN, PD), np.float32)
    for b in range(B):
        at = (b % GB) * S
        slots[b // GB, at + 2:at + S] = pt[b]
    patches = np.ascontiguousarray(slots.reshape(NT, TT, PC, P).transpose(3, 0, 2, 1))
    sel = np.zeros((ROWS, N), np.float32)
    for g in range(G):
        for n in range(GB * S):
            s = n % S
            for row in ([0], [1, 3], [2, 3 + s - 1])[min(s, 2)]:
                sel[row, g * GN + n] = 1.0
    rows = np.concatenate([a(cls_tok).reshape(1, E), a(L0_tok_cls_token).reshape(1, E),
                           a(L0_tok_b).reshape(1, E), a(L0_tok_pos_embed).reshape(S - 1, E)], 0)
    order = np.arange(E).reshape(2 * H0, D0 // 2, 2).transpose(0, 2, 1).reshape(E)
    wqkv = chunks(np.concatenate([a(L0_attn_Wq)[:, order], a(L0_attn_Wk)[:, order], a(L0_attn_Wv)], 1))
    lam = np.stack([a(L0_attn_lambda_q1), a(L0_attn_lambda_k1), a(L0_attn_lambda_q2), a(L0_attn_lambda_k2)])
    lam = np.ascontiguousarray(np.broadcast_to(lam.reshape(1, 2, 2, D0), (P, 2, 2, D0)))
    lnwb = np.stack([tiled(L0_attn_ln_w, P // (2 * D0)), tiled(L0_attn_ln_b, P // (2 * D0))], 1)
    part = np.arange(P)
    hmask = (part[:, None] // D1 == np.arange(HC)[None, :]).astype(np.float32)
    vmask = np.zeros((KR, KT, D1), np.float32)
    vones = np.zeros((KR, 2, KC, 2, KT, VW), np.float32)
    for j in range(KT):
        vmask[j * S:(j + 1) * S, j] = 1.0
        vones[j * S:(j + 1) * S, :, :, :, j, D1] = 1.0
    causal = np.where(np.tril(np.ones((S, S), bool)), 0.0, MASKED).astype(np.float32)
    rowsel = (part[None, :] % HALF == np.arange(S)[:, None]).astype(np.float32)
    w1 = np.ascontiguousarray(a(L1_ffn_W1).reshape(NX, EC, P, FF).transpose(2, 1, 0, 3))
    tie = np.arange(NX, 0, -1).astype(np.float32)
    tail = np.concatenate([a(L1_ffn_bo), a(L1_ffn_ln_gamma), a(L1_ffn_ln_beta), tie])
    tail = np.ascontiguousarray(np.broadcast_to(tail[None, :], (P, tail.size)))

    arrays = {
        "patches": patches, "tok_w": chunks(a(L0_tok_W).T), "rows": rows, "sel": sel, "wqkv": wqkv,
        "rope": rope_tables(), "lam": lam, "lnwb": lnwb, "wo0": chunks(L0_attn_Wo),
        "wf": chunks(a(L0_ffn_weight).T), "disha": tiled(L0_ffn_disha, 2), "wq1": chunks(a(L1_attn_q_proj).T),
        "wk1": chunks(a(L1_attn_k_proj).T), "wv1": chunks(a(L1_attn_v_proj).T),
        "wo1": chunks(a(L1_attn_o_proj).T), "hmask": hmask, "vmask": vmask, "vones": vones,
        "causal": causal, "rowsel": rowsel, "ident": np.eye(P, dtype=np.float32), "wr": chunks(L1_ffn_W_router),
        "w1": w1, "b1": a(L1_ffn_b1), "wo2": chunks(L1_ffn_Wo), "tail": tail,
    }
    nc = bacc.Bacc("TRN2", target_bir_lowering=False, num_devices=1)
    named, args = {}, []
    for name, v in arrays.items():
        v = np.ascontiguousarray(v)
        named[f"in_{name}"] = v
        args.append(nc.dram_tensor(f"in_{name}", v.shape, mybir.dt.from_np(v.dtype), kind="ExternalInput").ap())
    args.append(nc.dram_tensor("out_0", (N, E), F32, kind="ExternalOutput").ap())
    tower_kernel(nc, *args)
    res = run_bass_kernel_spmd(nc, [named], core_ids=[0])
    got = a(res.results[0]["out_0"]).reshape(G, GN, E)[:, 0:GB * S].reshape(B, S, E)
    return np.ascontiguousarray(got)
```

```python
from contextlib import ExitStack
import math

import numpy as np
import concourse.bass as bass
from concourse import mybir

F32 = mybir.dt.float32
F32R = mybir.dt.float32r
BF16 = mybir.dt.bfloat16
ALU = mybir.AluOpType
ACT = mybir.ActivationFunctionType
AX = mybir.AxisListType.X

P = 128
B, CIN, IMG, PATCH = 16, 3, 96, 16
NP = IMG // PATCH
PD = CIN * PATCH * PATCH
S = NP * NP + 2
E = 256
EC = E // P
PC = PD // P
G = 2
GB = B // G
TT = 102
GT = 3
GN = GT * TT
NT = G * GT
N = G * GN
H0, D0 = 8, 16
H1, D1 = 16, 16
HC = H1 // EC
KT = 3
KC = -(-H1 // KT)
KR = KT * S
VW = D1 + 1
NX = 4
FF = 1024
FC = FF // P
PAIRS = B // 2
HALF = 64
LAMBDA_INIT = 0.8 - 0.6 * math.exp(-0.3 * 12)
RMS_EPS, LN_EPS, LN_EPS_OUT = 1e-8, 1e-5, 1e-12
SCALE0 = 1.0 / D0 ** 0.25
SCALE1 = 1.0 / D1 ** 0.5
MASKED = -1e30
NORMS = 5
NV = 4
ROWS = 3 + NP * NP + 1


CONSTS = {"lam": 4 * D0, "lnwb": 2, "hmask": HC, "vmask": KT * D1, "causal": S, "rowsel": P, "ident": P}
ROUTE_FROM = PAIRS // G - 1
EARLY_CHUNKS = 2
TOK_LOADS = 3
WARM_UP = 9

QK_LATE = {1: (2, 3), 2: (0,)}
KEYS_LATE = {(1, 0): ((0, range(0, 4)),), (1, 1): ((0, range(4, 8)), (1, range(0, 2))), (2, 0): ((1, range(2, 8)),)}


def routes(slot):
    at = [2 * (t + t // GT) for t in range(NT)]
    return [(t, slot - at[t]) for t in reversed(range(NT)) if 0 <= slot - at[t] < 4]


def logits_by(slot):
    return sum(2 * (t + t // GT) + 2 <= slot for t in range(NT))


def slot_of(p, half):
    return 2 * (p - ROUTE_FROM) + half


def pairs_of(t):
    return (t // GT) * (PAIRS // G) + -(-min((t % GT + 1) * TT, GB * S) // (2 * S))


def tower_kernel(nc, patches, tok_w, rows_sel, const, wqkv, rope, w0, wq1, wk1, wv1, wo1, vones, wr, w1, b1,
                 low, wo2, tail, out):
    with ExitStack() as ctx:
        def sb(name, shape, dt=F32):
            return ctx.enter_context(nc.sbuf_tensor(name, shape, dt))

        def sem(name):
            return ctx.enter_context(nc.semaphore(name))

        bank = [ctx.enter_context(nc.psum_tensor(f"bank{i}", [P, 512], F32)) for i in range(8)]

        const_sb = sb("const_sb", [P, sum(CONSTS.values())])
        part, at = {}, 0
        for name, width in CONSTS.items():
            part[name] = const_sb[:, at:at + width]
            at += width
        lam_sb = part["lam"].rearrange("p (a b d) -> p a b d", a=2, b=2)
        lnwb_sb, hmask_sb, ident = part["lnwb"], part["hmask"], part["ident"]
        vmask_sb = part["vmask"][0:KR].rearrange("p (j e) -> p j e", j=KT)
        causal_f, rowsel_f = part["causal"][0:S], part["rowsel"][0:S]
        inputs = ExitStack()
        wq1_sb, wk1_sb, wv1_sb = (inputs.enter_context(nc.sbuf_tensor(name, [P, EC, E], F32))
                                  for name in ("wq1_sb", "wk1_sb", "wv1_sb"))
        x1T = inputs.enter_context(nc.sbuf_tensor("x1T", [P, EC, N], F32))
        inputs.close()
        wo2_lo = sb("wo2_lo", [P, FC, E], F32R)
        sb("spare", [P, 3 * EC * E + EC * N - FC * E])
        wo1_sb = sb("wo1_sb", [P, EC, E])
        causal_sb = sb("causal_sb", [S, S], BF16)
        rowsel_sb = sb("rowsel_sb", [S, P], BF16)
        identb = sb("identb", [P, P], BF16)
        wr_sb = sb("wr_sb", [P, EC, NX])
        w1_sb = sb("w1_sb", [P, EC, NX, FF])
        b1_sb = sb("b1_sb", [2 * NX, FF])
        b1_parts = sb("b1_parts", [2 * NX, FF], F32R)
        low_sb = sb("low_sb", [2 * NX, 2])
        wo2_sb = sb("wo2_sb", [P, FC, E])
        tail_sb = sb("tail_sb", [P, 3 * E + NX])
        bo_sb = tail_sb[:, 0:E]
        gamma_sb = tail_sb[:, E:2 * E]
        beta_sb = tail_sb[:, 2 * E:3 * E]
        tie_sb = tail_sb[:, 3 * E:3 * E + NX]
        expo = sb("expo", [P, 16])

        h = sb("h", [P, NT, E])
        xn = sb("xn", [P, NT, E])
        aT1 = sb("aT1", [P, EC, N])
        x3T = sb("x3T", [P, EC, N])
        stats = sb("stats", [P, NORMS, NT, 6])
        mean = sb("mean", [P, NORMS, NT, 2])
        vare = sb("vare", [P, NORMS, NT, 1])
        rstd = sb("rstd", [P, NORMS, NT, 1])
        lam_p = sb("lam_p", [P, 2, D0])
        lam_e = sb("lam_e", [P, 2])
        neg_lam = sb("neg_lam", [P, 1])
        lnwb_s = sb("lnwb_s", [P, 2])

        ms = sb("ms", [P, 2, 2, H0])
        smx = sb("smx", [P, 2, EC, HC])
        orc = sb("orc", [P, H1])

        lmax = sb("lmax", [P, 1])
        lcand = sb("lcand", [P, NX])
        oh = sb("oh", [P, 2, 2, NX], BF16)
        ohT = sb("ohT", [2 * NX, N], F32R)

        early = ExitStack()

        def sb_early(name, shape, dt=F32):
            return early.enter_context(nc.sbuf_tensor(name, shape, dt))

        tok_w_sb = sb_early("tok_w_sb", [P, PC, E])
        rows_sel_sb = sb_early("rows_sel_sb", [ROWS, E + N])
        rows_sb, sel_sb = rows_sel_sb[:, 0:E], rows_sel_sb[:, E:E + N]
        wqkv_sb = sb_early("wqkv_sb", [P, EC, 3 * E])
        rope_sb = sb_early("rope_sb", [P, NT, 2, D0])
        w0_sb = sb_early("w0_sb", [P, 2 * EC + 1, E])
        wo0_sb, wf_sb, disha_sb = w0_sb[:, 0:EC, :], w0_sb[:, EC:2 * EC, :], w0_sb[:, 2 * EC, :]
        still = sb_early("still", [P, 512], BF16)
        xT0 = sb_early("xT0", [P, EC, TT])
        xTf = sb_early("xTf", [P, EC, TT])
        km0 = sb_early("km0", [P, EC * GB * HC * S])
        prod = sb_early("prod", [P, 2, H0, H0, D0])
        prodv = prod[:, :, :, :, :].rearrange("p a n m d -> p (a n m d)").rearrange(
            "p (n e m) -> p n e m", n=H0, m=H0)
        qk = sb_early("qk", [P, 2 * E])
        qk_c = sb_early("qk_c", [P, 2 * E])
        qk_s = sb_early("qk_s", [P, 2 * E])
        v0 = sb_early("v0", [P, 2, E])
        s0 = sb_early("s0", [P, 2, H0, H0])
        small = sb_early("small", [P, 4, 2, H0])
        amix = sb_early("amix", [P, H0, H0])
        att = sb_early("att", [P, E])
        attsq = sb_early("attsq", [P, E])
        attn_n = sb_early("attn_n", [P, E])
        aT = sb_early("aT", [P, EC, TT])
        early.close()

        xm_hi = sb("xm_hi", [P, EC, NX, N], F32R)
        xm_lo = sb("xm_lo", [P, EC, NX, N], F32R)
        w_hi = sb("w_hi", [P, 2, EC * NX, P], F32R)
        w_lo = sb("w_lo", [P, 2, EC * NX, P], F32R)
        x3_hi = sb("x3_hi", [P, 2, EC, TT], F32R)
        x3_lo = sb("x3_lo", [P, 2, EC, TT])
        xbo = sb("xbo", [P, 2, E])
        hb = sb("hb", [P, 2, E])
        y = sb("y", [P, 2, E])
        yo = sb("yo", [P, 2, E])

        hT = sb("hT", [P, 2, GN])

        middle = ExitStack()

        def sb_middle(name, shape, dt=F32):
            return middle.enter_context(nc.sbuf_tensor(name, shape, dt))

        pool_b = sb_middle("pool_b", [P, FC * N])
        patches_sb = pool_b[:, 0:PC * N].rearrange("p (t c n) -> p t c n", t=NT, c=PC)
        km = [b[:, 0:EC * GB * HC * S].rearrange("p (c b h k) -> p c b h k", c=EC, b=GB, h=HC)
              for b in (km0, pool_b)]
        x3 = sb_middle("x3", [P, 2, 2, EC, KT, S])
        qT = sb_middle("qT", [P, G, EC, GN])
        vb = sb_middle("vb", [KR, 2, KC, 2, KT, VW])
        prob = sb_middle("prob", [P, 2, EC, HC, S])
        pT = sb_middle("pT", [KR, 2, KC, P])
        oc = sb_middle("oc", [P, 2, H1, VW])
        on = sb_middle("on", [P, 2, E])
        middle.close()

        hT_hi = sb("hT_hi", [P, FC, N], F32R)
        hT_lo = sb("hT_lo", [P, FC, N], F32R)
        wo2_hi = sb("wo2_hi", [P, FC, E], F32R)

        d_patch = [sem(f"d_patch{t}") for t in range(NT)]
        d_tok = [sem(f"d_tok{i}") for i in range(TOK_LOADS)]
        d_qkv = [sem(f"d_qkv{c}") for c in range(EC)]
        d_rows, d_rope, d_const, d_w0, d_l1 = (
            sem("d_rows"), sem("d_rope"), sem("d_const"), sem("d_w0"), sem("d_l1"))
        still_ready = sem("still_ready")
        d_w1, d_tail = sem("d_w1"), sem("d_tail")
        d_out = [sem("d_out0"), sem("d_out1")]
        s_setup = sem("s_setup")
        dve_setup = sem("dve_setup")
        s_lam = sem("s_lam")
        s_lame = sem("s_lame")
        s_v = sem("s_v")
        s_p = sem("s_p")
        proj_done, h_ready = sem("proj_done"), sem("h_ready")
        var_ready = [sem(f"var_ready{k}") for k in range(NORMS)]
        rstd_ready = [sem(f"rstd_ready{k}") for k in range(NORMS)]
        xn_ready = [sem(f"xn_ready{k}") for k in range(NORMS)]
        turned = [sem(f"turned{k}") for k in range(5)]
        copied = [sem(f"copied{k}") for k in range(5)]
        qkv_done, qkv_copied = sem("qkv_done"), sem("qkv_copied")
        rope_s_ready, rope_ready, prod1_ready = sem("rope_s_ready"), sem("rope_ready"), sem("prod1_ready")
        prodv_mine = sem("prodv_mine")
        s0_ready, p0_ready = sem("s0_ready"), sem("p0_ready")
        amix_ready, prodv_ready = sem("amix_ready"), sem("prodv_ready")
        att_ready, sq_ready, ms_ready, rms_ready = sem("att_ready"), sem("sq_ready"), sem("ms_ready"), sem("rms_ready")
        attn_ready = sem("attn_ready")
        wo_done, wo_added = sem("wo_done"), sem("wo_added")
        ffn_done, ffn_added = sem("ffn_done"), sem("ffn_added")
        wo1_done, wo1_added = sem("wo1_done"), sem("wo1_added")
        qk1_done, qk1_copied = sem("qk1_done"), sem("qk1_copied")
        keys_copied = sem("keys_copied")
        x3_ready = sem("x3_ready")
        v1_done, v1_copied = sem("v1_done"), sem("v1_copied")
        s1_done, s1_sub, p1_ready = sem("s1_done"), sem("s1_sub"), sem("p1_ready")
        pt_done, pt_copied_a, pt_copied_v = sem("pt_done"), sem("pt_copied_a"), sem("pt_copied_v")
        pv_done, pv_copied, on_ready = sem("pv_done"), sem("pv_copied"), sem("on_ready")
        ot_done, ot_copied = sem("ot_done"), sem("ot_copied")
        logit_done, oh_ready, ohb_done = sem("logit_done"), sem("oh_ready"), sem("ohb_done")
        xm_ready, ohT_copied = sem("xm_ready"), sem("ohT_copied")
        wo2_hi_ready, wo2_lo_ready, ff_split = sem("wo2_hi_ready"), sem("wo2_lo_ready"), sem("ff_split")
        w_hi_ready, w_lo_ready, b1_ready = sem("w_hi_ready"), sem("w_lo_ready"), sem("b1_ready")
        x3_split = sem("x3_split")
        ff_done, ff_ready, y_done = sem("ff_done"), sem("ff_ready"), sem("y_done")
        xbo_ready, hb_ready, yo_ready, y_taken = sem("xbo_ready"), sem("hb_ready"), sem("yo_ready"), sem("y_taken")

        def tile_cols(t):
            return slice(t * TT, (t + 1) * TT)

        def residual_bank(t):
            return bank[3] if t < NT - 1 else bank[5]

        def pair_cols(p, i):
            b = 2 * p + i
            at = (b // GB) * GN + (b % GB) * S
            return slice(at, at + S)

        block = ctx.enter_context(nc.Block())

        @block.sync
        def _(sp):
            sp.dma_start(patches_sb[:, 0], patches[:, 0]).then_inc(d_patch[0], 16)
            for i in range(TOK_LOADS):
                c = slice(i * PC // TOK_LOADS, (i + 1) * PC // TOK_LOADS)
                sp.dma_start(tok_w_sb[:, c], tok_w[:, c]).then_inc(d_tok[i], 16)
            sp.dma_start(rows_sel_sb[:], rows_sel).then_inc(d_rows, 16)
            sp.dma_start(const_sb[:], const).then_inc(d_const, 16)
            for c in range(EC):
                sp.dma_start(wqkv_sb[:, c], wqkv[:, c]).then_inc(d_qkv[c], 16)
            sp.dma_start(rope_sb[0:TT], rope).then_inc(d_rope, 16)
            sp.dma_start(patches_sb[:, 1], patches[:, 1]).then_inc(d_patch[1], 16)
            sp.dma_start(w0_sb[:], w0).then_inc(d_w0, 16)
            for t in range(2, NT):
                sp.dma_start(patches_sb[:, t], patches[:, t]).then_inc(d_patch[t], 16)
            for dst, src in ((wq1_sb, wq1), (wk1_sb, wk1), (wv1_sb, wv1), (wo1_sb, wo1), (vb, vones),
                             (wr_sb, wr), (b1_sb, b1), (low_sb, low)):
                sp.dma_start(dst[:], src).then_inc(d_l1, 16)
            sp.dma_start(w1_sb[:], w1).then_inc(d_w1, 16)
            sp.dma_start(wo2_sb[:], wo2).then_inc(d_w1, 16)
            sp.dma_start(tail_sb[:], tail).then_inc(d_tail, 16)
            for t in range(NT):
                sp.wait_ge(yo_ready, t + 1)
                sp.dma_start(out[tile_cols(t), :], yo[0:TT, t % 2, :]).then_inc(d_out[t % 2], 16)
            sp.wait_ge(d_out[0], 16 * (NT // 2))
            sp.wait_ge(d_out[1], 16 * (NT // 2))

        @block.tensor
        def _(pe):
            mm = nc.tensor.matmul

            def turn(k, t, src, psum, rows_=TT):
                for c in range(EC):
                    last = nc.tensor.transpose(psum[:, c * P:c * P + rows_], src[0:rows_, c * P:(c + 1) * P],
                                               ident[0:rows_, 0:rows_])
                last.then_inc(turned[k], 1)

            def keep_warm(n):
                for _ in range(n):
                    mm(bank[7][:, :], still[:, 0:P], still[:, :], start=True, stop=True)

            def project(t, chunks):
                if chunks[0] == 0:
                    pe.wait_ge(d_patch[t], 16)
                    if t:
                        pe.wait_ge(h_ready, t)
                for c in chunks:
                    if t == 0 and c % (PC // TOK_LOADS) == 0:
                        pe.wait_ge(d_tok[c * TOK_LOADS // PC], 16)
                    mm(bank[2][0:TT, 0:E], patches_sb[:, t, c, :], tok_w_sb[:, c, :], start=(c == 0), stop=False)
                if chunks[-1] == PC - 1:
                    if t == 0:
                        pe.wait_ge(d_rows, 16)
                    mm(bank[2][0:TT, 0:E], sel_sb[:, tile_cols(t)], rows_sb[:, :],
                       start=False, stop=True).then_inc(proj_done, 1)

            def to_qkv(t):
                pe.wait_ge(xn_ready[0], t + 1)
                if t:
                    pe.wait_ge(copied[0], t)
                turn(0, t, xn[:, t, :], bank[4])
                pe.wait_ge(copied[0], t + 1)
                if t:
                    pe.wait_ge(qkv_copied, 2 * t)
                for c in range(EC):
                    if t == 0:
                        pe.wait_ge(d_qkv[c], 16)
                    last = mm(bank[0][0:TT, :], xT0[:, c, :], wqkv_sb[:, c, 0:2 * E],
                              start=(c == 0), stop=(c == EC - 1))
                last.then_inc(qkv_done, 1)
                for c in range(EC):
                    last = mm(bank[1][0:TT, 0:E], xT0[:, c, :], wqkv_sb[:, c, 2 * E:3 * E],
                              start=(c == 0), stop=(c == EC - 1))
                last.then_inc(qkv_done, 1)

            def turn_attn(t):
                pe.wait_ge(attn_ready, t + 1)
                if t:
                    pe.wait_ge(copied[2], t)
                turn(1, t, attn_n, bank[5])

            def to_wo(t):
                o = residual_bank(t)
                pe.wait_ge(copied[1], t + 1)
                if t:
                    pe.wait_ge(ffn_added, t)
                else:
                    pe.wait_ge(d_w0, 16)
                    pe.wait_ge(s_setup, 1)
                for c in range(EC):
                    last = mm(o[0:TT, 0:E], aT[:, c, :], wo0_sb[:, c, :], start=(c == 0), stop=(c == EC - 1))
                last.then_inc(wo_done, 1)

            def to_ffn(t):
                o = residual_bank(t)
                pe.wait_ge(xn_ready[1], t + 1)
                turn(2, t, xn[:, t, :], bank[5])
                pe.wait_ge(copied[2], t + 1)
                pe.wait_ge(wo_added, t + 1)
                for c in range(EC):
                    last = mm(o[0:TT, 0:E], xTf[:, c, :], wf_sb[:, c, :], start=(c == 0), stop=(c == EC - 1))
                last.then_inc(ffn_done, 1)

            def to_second(t):
                pe.wait_ge(xn_ready[2], t + 1)
                if t:
                    pe.wait_ge(copied[3], t)
                turn(3, t, xn[:, t, :], bank[6])

            def qk_unit(g, i, o):
                w, c_out = (wq1_sb, i) if i < EC else (wk1_sb, i - EC)
                if g and i == EC:
                    pe.wait_ge(copied[3], NT)
                if g and i < EC:
                    pe.wait_ge(qk1_copied, 2 * EC + i)
                for c in range(EC):
                    last = mm(o[:, 0:GN], w[:, c, c_out * P:(c_out + 1) * P],
                              x1T[:, c, g * GN:(g + 1) * GN], start=(c == 0), stop=(c == EC - 1))
                last.then_inc(qk1_done, 1)

            def values(p):
                pe.wait_ge(x3_ready, p + 1)
                if p:
                    pe.wait_ge(v1_copied, p)
                for i in range(2):
                    for c in range(EC):
                        last = mm(bank[7][0:KR, i * E:(i + 1) * E],
                                  x3[:, p % 2, i, c, :, :].rearrange("p j k -> p (j k)"), wv1_sb[:, c, :],
                                  start=(c == 0), stop=(c == EC - 1))
                last.then_inc(v1_done, 1)

            def scores(p):
                g = 2 * p // GB
                pe.wait_ge(qk1_copied, 2 * EC * (g + 1) - 1)
                pe.wait_ge(keys_copied, 1)
                if p:
                    pe.wait_ge(s1_sub, p)
                for c in range(EC):
                    o = bank[c][:, 0:HC * S]
                    mm(o, rowsel_sb[:, :], causal_sb[:, :].unsqueeze(1).to_broadcast([S, HC, S]),
                       start=True, stop=False, skip_group_check=True)
                    for i in range(2):
                        b = (2 * p + i) % GB
                        last = mm(bank[c][HALF * i:HALF * i + S, 0:HC * S], qT[:, g, c, b * S:(b + 1) * S],
                                  km[g][:, c, b, :, :], start=False, stop=(i == 1), skip_group_check=True)
                last.then_inc(s1_done, 1)

            def turn_probs(p):
                pe.wait_ge(p1_ready, p + 1)
                if p:
                    pe.wait_ge(pv_copied, p)
                else:
                    pe.wait_ge(ffn_added, NT - 1)
                pf = prob[:, p % 2, :, :, :].rearrange("p c h k -> p (c h k)")
                for c in range(KC):
                    r = KR if c < KC - 1 else S
                    last = nc.tensor.transpose(bank[2 + c // 4][0:r, (c % 4) * P:(c % 4 + 1) * P],
                                               pf[:, c * KR:c * KR + r], ident[:, :])
                last.then_inc(pt_done, 1)

            def mix_values(p):
                pe.wait_ge(pt_copied_a, p + 1)
                pe.wait_ge(pt_copied_v, p + 1)
                pe.wait_ge(v1_copied, p + 1)
                for c in range(KC):
                    r, w = (KR, KT * VW) if c < KC - 1 else (S, VW)
                    at = (c % 4) * 2 * KT * VW
                    o = bank[2 + c // 4][0:HALF + S, at:at + 2 * KT * VW].rearrange("p (i w) -> p i w", i=2)
                    last = mm(o[:, :, 0:w], pT[0:r, p % 2, c, 0:HALF + S],
                              vb[0:r, p % 2, c, :, :, :].rearrange("p i j w -> p i (j w)")[:, :, 0:w],
                              start=True, stop=True)
                last.then_inc(pv_done, 1)

            def turn_mixed(p):
                pe.wait_ge(on_ready, p + 1)
                if p:
                    pe.wait_ge(ot_copied, p)
                if logits_by(slot_of(p, 1)):
                    pe.wait_ge(oh_ready, logits_by(slot_of(p, 1)))
                for c in range(EC):
                    last = nc.tensor.transpose(bank[4][:, c * P:(c + 1) * P], on[:, p % 2, c * P:(c + 1) * P],
                                               ident[:, :])
                last.then_inc(ot_done, 1)

            def route(t, step_):
                if step_ == 0:
                    pe.wait_ge(ot_copied, pairs_of(t))
                    if t == 0:
                        pe.wait_ge(qk1_copied, 2 * EC * G - 1)
                    if t:
                        pe.wait_ge(copied[4], t)
                    for c in range(EC):
                        last = mm(bank[5][0:TT, 0:E], aT1[:, c, tile_cols(t)], wo1_sb[:, c, :],
                                  start=(c == 0), stop=(c == EC - 1))
                    last.then_inc(wo1_done, 1)
                elif step_ == 1:
                    pe.wait_ge(xn_ready[3], t + 1)
                    turn(4, t, xn[:, t, :], bank[5])
                elif step_ == 2:
                    pe.wait_ge(copied[4], t + 1)
                    pe.wait_ge(ot_copied, min(t + t // GT + 1 + ROUTE_FROM, PAIRS))
                    if t:
                        pe.wait_ge(oh_ready, t)
                    for c in range(EC):
                        last = mm(bank[4][0:TT, 0:NX], x3T[:, c, tile_cols(t)], wr_sb[:, c, :],
                                  start=(c == 0), stop=(c == EC - 1))
                    last.then_inc(logit_done, 1)
                else:
                    pe.wait_ge(oh_ready, t + 1)
                    if t:
                        pe.wait_ge(xm_ready, t)
                        pe.wait_ge(ohT_copied, t)
                    for e in range(NX):
                        mm(bank[6][:, e * TT:(e + 1) * TT], oh[0:TT, t % 2, 0, e:e + 1].to_broadcast([TT, P]),
                           identb[0:TT, 0:TT], start=True, stop=True)
                    mm(bank[6][0:2 * NX, NX * TT:NX * TT + TT],
                       oh[0:TT, t % 2, :, :].rearrange("p a x -> p (a x)"), identb[0:TT, 0:TT],
                       start=True, stop=True).then_inc(ohb_done, 1)

            pe.wait_ge(still_ready, 1)
            keep_warm(WARM_UP)
            project(0, range(PC))
            keep_warm(WARM_UP)
            pe.wait_ge(d_const, 16)
            for t in range(-1, NT + 2):
                if t < 1:
                    to_qkv(t + 1)
                if t == NT - 1:
                    pe.wait_ge(qkv_copied, 2 * NT)
                    qk_unit(0, EC + 1, bank[4])
                    qk_unit(0, 1, bank[0])
                if 3 <= t + 3 < NT:
                    project(t + 3, range(PC))
                if 1 <= t <= NT:
                    turn_attn(t - 1)
                    to_wo(t - 1)
                if t >= 2:
                    to_second(t - 2)
                if 0 <= t < NT - 2:
                    to_qkv(t + 2)
                if t == NT - 1:
                    scores(0)
                if t == NT:
                    values(0)
                    turn_probs(0)
                    scores(1)
                if t == -1:
                    project(1, range(PC))
                    project(2, range(PC))
                if 1 <= t <= NT:
                    to_ffn(t - 1)
                if t == NT:
                    values(1)
                    mix_values(0)
                if t == NT - 2:
                    pe.wait_ge(d_l1, 16 * 8)
                    pe.wait_ge(copied[3], GT)
                    qk_unit(0, EC, bank[7])
                    qk_unit(0, 0, bank[2])

            def experts(g, f):
                n = g * FC + f
                cols = slice(g * GN, (g + 1) * GN)
                if f == 0:
                    pe.wait_ge(xm_ready, GT * (g + 1))
                    pe.wait_ge(ohT_copied, GT * (g + 1))
                if n >= 2:
                    pe.wait_ge(ff_ready, n - 1)
                if n == 0:
                    pe.wait_ge(b1_ready, 1)
                o = bank[n % 2][:, 0:GN]
                mm(o, b1_parts[:, f * P:(f + 1) * P], ohT[:, cols], start=True, stop=False)
                for w, x in ((w_hi, xm_hi), (w_hi, xm_lo), (w_lo, xm_hi)):
                    if w is w_hi:
                        pe.wait_ge(w_hi_ready, n + 1)
                    else:
                        pe.wait_ge(w_lo_ready, n + 1)
                    for e in range(NX):
                        for c in range(EC):
                            last = mm(o, w[:, n % 2, c * NX + e, :], x[:, c, e, cols], start=False,
                                      stop=(w is w_lo and e == NX - 1 and c == EC - 1))
                last.then_inc(ff_done, 1)

            def down(t):
                pe.wait_ge(wo2_lo_ready, FC // 2)
                if t >= 2:
                    pe.wait_ge(y_taken, t - 1)
                for f in range(FC):
                    if f == 0:
                        pe.wait_ge(ff_ready, FC * (t // GT + 1) - 1)
                        pe.wait_ge(ff_split, FC * (t // GT + 1) - 1)
                    elif f == FC - 1:
                        pe.wait_ge(ff_ready, FC * (t // GT + 1))
                        pe.wait_ge(ff_split, FC * (t // GT + 1))
                    for x, w in ((hT_hi, wo2_hi), (hT_hi, wo2_lo), (hT_lo, wo2_hi)):
                        last = mm(bank[2 + t % 2][0:TT, 0:E], x[:, f, tile_cols(t)], w[:, f, :],
                                  start=(f == 0 and w is wo2_hi and x is hT_hi), stop=(f == FC - 1 and x is hT_lo))
                last.then_inc(y_done, 1)

            for p in range(1, PAIRS):
                ahead = p < PAIRS - 1
                if ahead:
                    scores(p + 1)
                for t, step_ in routes(slot_of(p - 1, 1)):
                    route(t, step_)
                turn_probs(p)
                if ahead:
                    values(p + 1)
                for i in QK_LATE.get(p, ()):
                    qk_unit(1, i, bank[5 + i % 2])
                turn_mixed(p - 1)
                for t, step_ in routes(slot_of(p, 0)):
                    route(t, step_)
                if p == PAIRS - 1:
                    pe.wait_ge(d_w1, 32)
                    experts(0, 0)
                mix_values(p)
                if p == 2:
                    qk_unit(1, 1, bank[6])
            experts(0, 1)
            for t, step_ in routes(slot_of(PAIRS - 1, 1)):
                route(t, step_)
            turn_mixed(PAIRS - 1)
            for t, step_ in routes(slot_of(PAIRS, 0)):
                route(t, step_)

            for f in range(EARLY_CHUNKS, FC):
                experts(0, f)
                for t, step_ in routes(slot_of(PAIRS, 0) + f - EARLY_CHUNKS + 1):
                    route(t, step_)
            for f in range(FC):
                experts(1, f)
                if f % 2 and f // 2 < GT:
                    down(f // 2)
            for t in range(GT, NT):
                down(t)

        @block.scalar
        def _(act):
            fn = nc.scalar.activation

            def turn_out(k, t, psum, dst, **affine):
                act.wait_ge(turned[k], t + 1)
                fn(dst, psum[:, 0:EC * P].rearrange("p (c n) -> p c n", c=EC)[:, :, 0:TT],
                   ACT.Identity if affine else ACT.Copy, **affine).then_inc(copied[k], 1)

            def h_copy(t):
                act.wait_ge(proj_done, t + 1)
                fn(h[0:TT, t, :], bank[2][0:TT, 0:E], ACT.Copy).then_inc(h_ready, 1)

            def squares(t):
                act.wait_ge(att_ready, t + 1)
                fn(attsq[0:TT, :], att[0:TT, :], ACT.Square).then_inc(sq_ready, 1)

            def qk_out(t):
                act.wait_ge(qkv_done, 2 * t + 1)
                if t >= 1:
                    act.wait_ge(rope_ready, t)
                fn(qk[0:TT, :], bank[0][0:TT, :], ACT.Copy).then_inc(qkv_copied, 1)

            def v_out(t):
                act.wait_ge(qkv_done, 2 * t + 2)
                if t >= 2:
                    act.wait_ge(prodv_ready, t - 1)
                    act.wait_ge(att_ready, t - 1)
                fn(v0[0:TT, t % 2, :], bank[1][0:TT, 0:E], ACT.Copy).then_inc(qkv_copied, 1)

            def exps(t):
                act.wait_ge(s0_ready, t + 1)
                fn(s0[0:TT], s0[0:TT], ACT.Exp, scale=SCALE0).then_inc(p0_ready, 1)

            def queries_out(g, c, psum, n):
                act.wait_ge(qk1_done, n)
                fn(qT[:, g, c, :], psum[:, 0:GN], ACT.Copy).then_inc(qk1_copied, 1)

            def keys_out(g, c, psum, n, heads=range(HC)):
                act.wait_ge(qk1_done, n)
                src = psum[:, 0:GB * S].rearrange("p (b k) -> p b k", b=GB)
                for j in heads:
                    last = fn(km[g][:, c, :, j, :], src, ACT.Copy, scale=hmask_sb[:, j:j + 1])
                if HC - 1 in heads:
                    last.then_inc(qk1_copied, 1)

            def probs(p):
                act.wait_ge(s1_sub, p + 1)
                x = prob[:, p % 2, :, :, :]
                fn(x, x, ACT.Exp, scale=SCALE1).then_inc(p1_ready, 1)

            def probs_out(p):
                act.wait_ge(pt_done, p + 1)
                if p >= 2:
                    act.wait_ge(pv_done, p - 1)
                fn(pT[:, p % 2, 0:4, :], bank[2][0:KR, :].rearrange("p (c n) -> p c n", c=4),
                   ACT.Copy).then_inc(pt_copied_a, 1)

            def mixed_out(p):
                act.wait_ge(pv_done, p + 1)
                if p >= 2:
                    act.wait_ge(on_ready, p - 1)
                for i in range(2):
                    rows_ = slice(HALF * i, HALF * i + S)
                    o = bank[2][rows_, 0:8 * KT * VW].rearrange("p (c i w) -> p c i w", c=4, i=2)
                    fn(oc[rows_, p % 2, 0:4 * KT, :].rearrange("p (c j) w -> p c (j w)", c=4), o[:, :, i, :], ACT.Copy)
                    at = i * KT * VW
                    fn(oc[rows_, p % 2, 4 * KT:5 * KT, :].rearrange("p j w -> p (j w)"),
                       bank[3][rows_, at:at + KT * VW], ACT.Copy)
                    at += 2 * KT * VW
                    last = fn(oc[rows_, p % 2, 5 * KT, :], bank[3][rows_, at:at + VW], ACT.Copy)
                last.then_inc(pv_copied, 1)

            def mixed_turned(p):
                act.wait_ge(ot_done, p + 1)
                at = pair_cols(p, 0).start
                fn(aT1[:, :, at:at + 2 * S].rearrange("p c (i n) -> p c i n", i=2),
                   bank[4][:, 0:EC * P].rearrange("p (c i n) -> p c i n", c=EC, i=2)[:, :, :, 0:S],
                   ACT.Copy).then_inc(ot_copied, 1)

            def route(t, step_):
                if step_ == 1:
                    turn_out(4, t, bank[5], x3T[:, :, tile_cols(t)])
                elif step_ == 3:
                    act.wait_ge(ohb_done, t + 1)
                    fn(ohT[:, tile_cols(t)], bank[6][0:2 * NX, NX * TT:NX * TT + TT], ACT.Copy).then_inc(ohT_copied, 1)

            def weights_up(n):
                if n >= 2:
                    act.wait_ge(ff_done, n - 1)
                f = n % FC
                fn(w_hi[:, n % 2, :, :], w1_sb[:, :, :, f * P:(f + 1) * P].rearrange("p c x n -> p (c x) n"),
                   ACT.Copy).then_inc(w_hi_ready, 1)

            act.wait_ge(s_lam, 1)
            fn(lam_e[:, :], lam_e[:, :], ACT.Exp).then_inc(s_lame, 1)
            h_copy(0)
            for t in range(-1, NT + 2):
                if t == -1:
                    turn_out(0, 0, bank[4], xT0[:, :, :])
                    qk_out(0)
                    v_out(0)
                if 0 <= t < NT:
                    exps(t)
                if t == 0:
                    turn_out(0, 1, bank[4], xT0[:, :, :])
                    qk_out(1)
                    v_out(1)
                if 1 <= t <= NT:
                    if t == 1:
                        act.wait_ge(dve_setup, 1)
                    turn_out(1, t - 1, bank[5], aT[:, :, :], scale=lnwb_s[:, 0:1], bias=lnwb_s[:, 1:2])
                if t == NT - 1:
                    queries_out(0, 0, bank[2], 2)
                    keys_out(0, 0, bank[7], 1)
                    queries_out(0, 1, bank[0], 2 * EC)
                if 3 <= t + 3 < NT:
                    h_copy(t + 3)
                if t >= 2:
                    turn_out(3, t - 2, bank[6], x1T[:, :, tile_cols(t - 2)])
                if 0 <= t < NT - 2:
                    turn_out(0, t + 2, bank[4], xT0[:, :, :])
                if 0 <= t < NT:
                    squares(t)
                if 0 <= t < NT - 2:
                    qk_out(t + 2)
                if t == NT:
                    probs(0)
                    probs_out(0)
                if t == -1:
                    h_copy(1)
                    h_copy(2)
                if 0 <= t < NT - 2:
                    v_out(t + 2)
                if 1 <= t <= NT:
                    turn_out(2, t - 1, bank[5], xTf[:, :, :])
                if t == NT:
                    probs(1)

            def experts(g, f):
                n = g * FC + f
                act.wait_ge(ff_done, n + 1)
                fn(hT_hi[:, f, g * GN:(g + 1) * GN], bank[n % 2][:, 0:GN], ACT.Gelu)
                if n >= 2:
                    act.wait_ge(ff_split, n - 1)
                fn(hT[:, n % 2, :], bank[n % 2][:, 0:GN], ACT.Gelu).then_inc(ff_ready, 1)
                if n >= 2 and 2 * (n - 2) < FC:
                    two = slice(2 * (n - 2), 2 * (n - 1))
                    fn(wo2_hi[:, two, :], wo2_sb[:, two, :], ACT.Copy).then_inc(wo2_hi_ready, 1)

            mixed_out(0)
            for p in range(1, PAIRS):
                for t, step_ in routes(slot_of(p - 1, 1)):
                    route(t, step_)
                probs_out(p)
                if p < PAIRS - 1:
                    probs(p + 1)
                for c, heads in KEYS_LATE.get((p, 0), ()):
                    keys_out(1, c, bank[5 + c], 2 * EC + c + 1, heads)
                mixed_turned(p - 1)
                for t, step_ in routes(slot_of(p, 0)):
                    route(t, step_)
                if p == PAIRS - 1:
                    weights_up(1)
                    experts(0, 0)
                mixed_out(p)
                for c, heads in KEYS_LATE.get((p, 1), ()):
                    keys_out(1, c, bank[5 + c], 2 * EC + c + 1, heads)
                if p == PAIRS - 2:
                    act.wait_ge(d_w1, 32)
                    weights_up(0)
                if p == 2:
                    for c in range(EC):
                        queries_out(1, c, bank[5 + c], 3 * EC + c + 1)
            weights_up(2)
            experts(0, 1)
            for t, step_ in routes(slot_of(PAIRS - 1, 1)):
                route(t, step_)
            mixed_turned(PAIRS - 1)
            for t, step_ in routes(slot_of(PAIRS, 0)):
                route(t, step_)

            for f in range(EARLY_CHUNKS, FC):
                weights_up(f + 1)
                experts(0, f)
                for t, step_ in routes(slot_of(PAIRS, 0) + f - EARLY_CHUNKS + 1):
                    route(t, step_)
            for f in range(FC):
                if f + 1 < FC:
                    weights_up(FC + f + 1)
                experts(1, f)

        @block.vector
        def _(dve):
            tt, ts, red = nc.vector.tensor_tensor, nc.vector.tensor_scalar, nc.vector.tensor_reduce
            count = [0]
            r = slice(0, TT)

            def mark(ins):
                count[0] += 1
                ins.then_inc(s_v, 1)
                return count[0]

            def need(n):
                dve.wait_ge(s_v, n)

            def step(ins):
                need(mark(ins))

            def moments_1(k, t, src):
                return mark(nc.vector.bn_stats(stats[r, k, t, :], src))

            def moments_2(k, t, n):
                need(n)
                return mark(nc.vector.bn_aggr(mean[r, k, t, :], stats[r, k, t, :]))

            def moments_3(k, t, n, eps):
                need(n)
                ts(vare[r, k, t, :], mean[r, k, t, 1:2], eps, None, ALU.add).then_inc(var_ready[k], 1)

            def moments(k, t, src, eps):
                moments_3(k, t, moments_2(k, t, moments_1(k, t, src)), eps)

            def normed(k, t, src, dst):
                dve.wait_ge(rstd_ready[k], t + 1)
                ts(dst, src, mean[r, k, t, 0:1], rstd[r, k, t, :], ALU.subtract, ALU.mult).then_inc(xn_ready[k], 1)

            def prepare():
                dve.wait_ge(d_const, 16)
                step(tt(lam_p[:], lam_sb[:, :, 0, :], lam_sb[:, :, 1, :], ALU.mult))
                red(lam_e[:, :], lam_p[:], AX, ALU.add).then_inc(s_lam, 1)
                step(ts(lnwb_s[:, :], lnwb_sb[:, :], 1.0 - LAMBDA_INIT, None, ALU.mult))
                dve.wait_ge(s_lame, 1)
                step(tt(neg_lam[:], lam_e[:, 1:2], lam_e[:, 0:1], ALU.subtract))
                step(ts(neg_lam[:], neg_lam[:], -LAMBDA_INIT, None, ALU.add))
                nc.vector.memset(oc[:], 1.0).then_inc(dve_setup, 1)

            def halves(x):
                return x.rearrange("p (n a d) -> p n a d", n=H0, a=2)

            q, k_ = halves(qk_c[r, 0:E]), halves(qk_c[r, E:2 * E])
            av = att[r, :].rearrange("p (n e) -> p n e", n=H0)
            mx, sm, rc = (small[r, i] for i in range(3))

            def added(k, t, done, psum, gone):
                dve.wait_ge(done, t + 1)
                tt(h[r, t, :], h[r, t, :], psum[r, 0:E], ALU.add).then_inc(gone, 1)
                dve.wait_ge(gone, t + 1)
                moments(k, t, h[r, t, :], LN_EPS)

            def softmax_in(p):
                dve.wait_ge(s1_done, p + 1)
                if p >= 2:
                    dve.wait_ge(pt_done, p - 1)
                for c in range(EC):
                    sc = bank[c][:, 0:HC * S].rearrange("p (h k) -> p h k", h=HC)
                    m = smx[:, p % 2, c, :]
                    step(red(m, sc, AX, ALU.max))
                    last = tt(prob[:, p % 2, c], sc, m.unsqueeze(2).to_broadcast([P, HC, S]), ALU.subtract)
                last.then_inc(s1_sub, 1)

            def values(p):
                dve.wait_ge(v1_done, p + 1)
                if p >= 2:
                    dve.wait_ge(pv_done, p - 1)
                nf = KC - 1
                for i in range(2):
                    src = bank[7][0:KR, i * E:i * E + nf * KT * D1].rearrange("p (c j e) -> p c j e", c=nf, j=KT)
                    tt(vb[:, p % 2, 0:nf, i, :, 0:D1], src, vmask_sb[:, :, :].unsqueeze(1).to_broadcast([KR, nf, KT, D1]),
                       ALU.mult)
                    last = nc.vector.tensor_copy(vb[0:S, p % 2, nf, i, 0, 0:D1],
                                                 bank[7][0:S, i * E + nf * KT * D1:(i + 1) * E])
                last.then_inc(v1_copied, 1)

            def scaled(t):
                dve.wait_ge(rms_ready, t + 1)
                tt(attn_n[r, :].rearrange("p (n e) -> p n e", n=H0), av,
                   ms[r, t % 2, 1, :].unsqueeze(2).to_broadcast([TT, H0, 2 * D0]), ALU.mult).then_inc(attn_ready, 1)

            def rope_cos(t):
                dve.wait_ge(qkv_copied, 2 * t + 1)
                if t == 0:
                    dve.wait_ge(d_rope, 16)
                cos = rope_sb[r, t, 0, :].unsqueeze(1).to_broadcast([TT, 4 * H0, D0])
                return mark(tt(qk_c[r, :].rearrange("p (g d) -> p g d", d=D0),
                               qk[r, :].rearrange("p (g d) -> p g d", d=D0), cos, ALU.mult))

            def rope_sum(t, n):
                need(n)
                dve.wait_ge(rope_s_ready, t + 1)
                tt(qk_c[r, :], qk_c[r, :], qk_s[r, :], ALU.add).then_inc(rope_ready, 1)

            def squares_sum(t):
                dve.wait_ge(sq_ready, t + 1)
                return mark(red(ms[r, t % 2, 0, :], attsq[r, :].rearrange("p (n e) -> p n e", n=H0), AX, ALU.add))

            def squares_mean(t, n):
                need(n)
                ts(ms[r, t % 2, 0, :], ms[r, t % 2, 0, :], 1.0 / (2 * D0), RMS_EPS,
                   ALU.mult, ALU.add).then_inc(ms_ready, 1)

            def keys_out():
                dve.wait_ge(qk1_done, EC + 1)
                for b in range(GB):
                    last = tt(km[0][:, 1, b, :, :],
                              bank[4][:, b * S:(b + 1) * S].unsqueeze(1).to_broadcast([P, HC, S]),
                              hmask_sb.unsqueeze(2).to_broadcast([P, HC, S]), ALU.mult)
                last.then_inc(keys_copied, 1)

            def attend(t):
                here, before, older = 0 <= t < NT, 1 <= t <= NT, t >= 2
                first, second = t < 1, 1 <= t < NT - 2
                if here:
                    dve.wait_ge(rope_ready, t + 1)
                    n = mark(tt(prod[r, 0], q[:, :, 0, :].unsqueeze(2).to_broadcast([TT, H0, H0, D0]),
                                k_[:, :, 0, :].unsqueeze(1).to_broadcast([TT, H0, H0, D0]), ALU.mult))
                if 2 <= t <= NT:
                    normed(1, t - 2, h[r, t - 2, :], xn[r, t - 2, :])
                if before:
                    squared = squares_sum(t - 1)
                if first:
                    dve.wait_ge(h_ready, t + 2)
                    m = moments_1(0, t + 1, h[r, t + 1, :])
                if here:
                    need(n)
                    n = mark(red(s0[r, 0], prod[r, 0], AX, ALU.add))
                if before:
                    squares_mean(t - 1, squared)
                if t == NT:
                    scaled(t - 1)
                if first:
                    m = moments_2(0, t + 1, m)
                if second:
                    dve.wait_ge(h_ready, t + 3)
                    m0 = moments_1(0, t + 2, h[r, t + 2, :])
                if first:
                    moments_3(0, t + 1, m, LN_EPS)
                if here:
                    dve.wait_ge(prod1_ready, t + 1)
                    need(n)
                    n = mark(red(s0[r, 1], prod[r, 1], AX, ALU.add))
                if first:
                    normed(0, t + 1, h[r, t + 1, :], xn[r, t + 1, :])
                if older:
                    dve.wait_ge(ffn_done, t - 1)
                    tt(h[r, t - 2, :], h[r, t - 2, :], residual_bank(t - 2)[r, 0:E], ALU.add).then_inc(ffn_added, 1)
                if here:
                    need(n)
                    n = mark(red(mx, s0[r], AX, ALU.max))
                if older:
                    dve.wait_ge(ffn_added, t - 1)
                    m2 = moments_1(2, t - 2, h[r, t - 2, :])
                if here:
                    need(n)
                    tt(s0[r], s0[r], mx.unsqueeze(3).to_broadcast([TT, 2, H0, H0]), ALU.subtract).then_inc(s0_ready, 1)
                if second:
                    m0 = moments_2(0, t + 2, m0)
                if older:
                    m2 = moments_2(2, t - 2, m2)
                if second:
                    moments_3(0, t + 2, m0, LN_EPS)
                if older:
                    moments_3(2, t - 2, m2, LN_EPS)
                if 1 <= t < NT - 1:
                    rope = rope_cos(t + 1)
                if here:
                    dve.wait_ge(p0_ready, t + 1)
                    n = mark(red(sm, s0[r], AX, ALU.add))
                if 1 <= t < NT:
                    scaled(t - 1)
                if here:
                    need(n)
                    n = mark(nc.vector.reciprocal(rc, sm))
                if second:
                    normed(0, t + 2, h[r, t + 2, :], xn[r, t + 2, :])
                if here:
                    need(n)
                    n = mark(ts(rc[:, 1, :], rc[:, 1, :], neg_lam[r, :], None, ALU.mult))
                if older:
                    normed(2, t - 2, h[r, t - 2, :], xn[r, t - 2, :])
                if t == NT:
                    dve.wait_ge(d_l1, 16 * 8)
                    softmax_in(0)
                if here:
                    need(n)
                    step(tt(s0[r], s0[r], rc.unsqueeze(3).to_broadcast([TT, 2, H0, H0]), ALU.mult))
                    dve.wait_ge(qkv_copied, 2 * t + 2)
                    tt(amix[r], s0[r, 0], s0[r, 1], ALU.add).then_inc(amix_ready, 1)
                    dve.wait_ge(amix_ready, t + 1)
                    if before:
                        dve.wait_ge(attn_ready, t)
                    tt(prodv[r, 0:NV], amix[r, 0:NV].unsqueeze(2).to_broadcast([TT, NV, 2 * D0, H0]),
                       v0[r, t % 2, :].rearrange("p (m e) -> p e m", m=H0).unsqueeze(1)
                       .to_broadcast([TT, NV, 2 * D0, H0]), ALU.mult).then_inc(prodv_mine, 1)
                if here:
                    dve.wait_ge(prodv_mine, t + 1)
                    red(av[:, 0:NV, :], prodv[r, 0:NV], AX, ALU.add)
                if t == NT - 1:
                    keys_out()
                if before:
                    dve.wait_ge(wo_done, t)
                    tt(h[r, t - 1, :], h[r, t - 1, :], residual_bank(t - 1)[r, 0:E], ALU.add).then_inc(wo_added, 1)
                if t == 0:
                    dve.wait_ge(h_ready, t + 3)
                    m0 = moments_1(0, t + 2, h[r, t + 2, :])
                if t < 1:
                    rope = rope_cos(t + 1)
                if t == 0:
                    m0 = moments_2(0, t + 2, m0)
                if 1 <= t < NT - 1:
                    rope_sum(t + 1, rope)
                if before:
                    dve.wait_ge(wo_added, t)
                    m = moments_1(1, t - 1, h[r, t - 1, :])
                if here:
                    dve.wait_ge(prodv_ready, t + 1)
                    red(av[:, NV:H0, :], prodv[r, NV:H0], AX, ALU.add).then_inc(att_ready, 1)
                if before:
                    m = moments_2(1, t - 1, m)
                if before:
                    moments_3(1, t - 1, m, LN_EPS)
                if t == 0:
                    moments_3(0, t + 2, m0, LN_EPS)
                if t < 1:
                    rope_sum(t + 1, rope)
                if t == 0:
                    normed(0, t + 2, h[r, t + 2, :], xn[r, t + 2, :])
                if t == NT:
                    normed(1, t - 1, h[r, t - 1, :], xn[r, t - 1, :])
                    values(0)

            def probs_out(p):
                dve.wait_ge(pt_done, p + 1)
                nc.vector.tensor_copy(pT[:, p % 2, 4, :], bank[3][0:KR, 0:P])
                nc.vector.tensor_copy(pT[0:S, p % 2, 5, :], bank[3][0:S, P:2 * P]).then_inc(pt_copied_v, 1)

            def mixed(p):
                dve.wait_ge(pv_copied, p + 1)
                if p >= 2:
                    dve.wait_ge(ot_done, p - 1)
                if p:
                    dve.wait_ge(on_ready, p)
                step(nc.vector.reciprocal(orc[:, :], oc[:, p % 2, :, D1]))
                tt(on[:, p % 2, :].rearrange("p (h e) -> p h e", h=H1), oc[:, p % 2, :, 0:D1],
                   orc[:, :].unsqueeze(2).to_broadcast([P, H1, D1]), ALU.mult).then_inc(on_ready, 1)

            def route(t, step_):
                if step_ == 0:
                    added(3, t, wo1_done, bank[5], wo1_added)
                elif step_ == 1:
                    normed(3, t, h[r, t, :], xn[r, t, :])
                elif step_ == 2:
                    dve.wait_ge(logit_done, t + 1)
                    step(red(lmax[r, :], bank[4][r, 0:NX], AX, ALU.max))
                    step(nc.vector.scalar_tensor_tensor(out=lcand[r, :], in0=bank[4][r, 0:NX], scalar=lmax[r, :],
                                                        in1=tie_sb[r, :], op0=ALU.is_equal, op1=ALU.mult))
                    step(red(lmax[r, :], lcand[r, :], AX, ALU.max))
                    ts(oh[r, t % 2, 0, :], lcand[r, :], lmax[r, :], None, ALU.is_equal)
                    ts(oh[r, t % 2, 1, :], lcand[r, :], lmax[r, :], None, ALU.is_equal).then_inc(oh_ready, 1)
                    dve.wait_ge(oh_ready, t + 1)
                else:
                    dve.wait_ge(ohT_copied, t + 1)
                    dve.wait_ge(x3_split, t + 1)
                    for x, src in ((xm_hi, x3_hi[:].bitcast(F32)), (xm_lo, x3_lo)):
                        for c in range(EC):
                            last = tt(x[:, c, :, tile_cols(t)],
                                      bank[6][:, 0:NX * TT].rearrange("p (x n) -> p x n", x=NX),
                                      src[:, t % 2, c, :].unsqueeze(1).to_broadcast([P, NX, TT]), ALU.mult)
                    last.then_inc(xm_ready, 1)

            def bias_parts():
                step(nc.vector.tensor_copy(b1_parts[:, :], b1_sb[:, :]))
                step(ts(b1_sb[:, :], b1_sb[:, :], low_sb[:, 0:1], None, ALU.mult))
                nc.vector.scalar_tensor_tensor(out=b1_parts[:, :], in0=b1_parts[:, :].bitcast(F32),
                                               scalar=low_sb[:, 1:2], in1=b1_sb[:, :],
                                               op0=ALU.mult, op1=ALU.add).then_inc(b1_ready, 1)

            def weights_low(n):
                dve.wait_ge(w_hi_ready, n + 1)
                f = n % FC
                tt(w_lo[:, n % 2, :, :], w1_sb[:, :, :, f * P:(f + 1) * P].rearrange("p c x n -> p (c x) n"),
                   w_hi[:, n % 2, :, :].bitcast(F32), ALU.subtract).then_inc(w_lo_ready, 1)

            nc.vector.memset(still[:, :], 0.0).then_inc(still_ready, 1)
            prepare()
            for t in range(-1, NT + 2):
                attend(t)
                if t == NT:
                    probs_out(0)
                    softmax_in(1)
            values(1)
            mixed(0)
            bias_parts()
            for p in range(1, PAIRS):
                ahead = p < PAIRS - 1
                if ahead:
                    softmax_in(p + 1)
                if p == ROUTE_FROM:
                    dve.wait_ge(d_tail, 16)
                probs_out(p)
                for t, step_ in routes(slot_of(p - 1, 1)):
                    if step_ == 3:
                        route(t, step_)
                if ahead:
                    values(p + 1)
                else:
                    weights_low(0)
                for t, step_ in routes(slot_of(p, 0)):
                    route(t, step_)
                if p == PAIRS - 1:
                    weights_low(1)
                for t, step_ in routes(slot_of(p, 1)):
                    if step_ == 1:
                        route(t, step_)
                mixed(p)
            weights_low(2)
            for t, step_ in routes(slot_of(PAIRS, 0)):
                route(t, step_)

            def finish(t):
                dve.wait_ge(y_done, t + 1)
                dve.wait_ge(xbo_ready, t + 1)
                tt(y[r, t % 2, :], bank[2 + t % 2][r, 0:E], xbo[r, t % 2, :], ALU.add).then_inc(y_taken, 1)
                dve.wait_ge(y_taken, t + 1)
                moments(4, t, y[r, t % 2, :], LN_EPS_OUT)
                normed(4, t, y[r, t % 2, :], y[r, t % 2, :])
                dve.wait_ge(xn_ready[4], t + 1)
                step(tt(y[r, t % 2, :], y[r, t % 2, :], gamma_sb[r, :], ALU.mult))
                dve.wait_ge(hb_ready, t + 1)
                if t >= 2:
                    dve.wait_ge(d_out[t % 2], 16 * (t // 2))
                tt(yo[r, t % 2, :], y[r, t % 2, :], hb[r, t % 2, :], ALU.add).then_inc(yo_ready, 1)
                dve.wait_ge(yo_ready, t + 1)

            for f in range(EARLY_CHUNKS, FC):
                weights_low(f + 1)
                for t, step_ in routes(slot_of(PAIRS, 0) + f - EARLY_CHUNKS + 1):
                    route(t, step_)
            for f in range(FC):
                if f + 1 < FC:
                    weights_low(FC + f + 1)
                if f % 2 == 0 and 2 <= f and f // 2 - 1 < GT:
                    finish(f // 2 - 1)
            for t in range(GT, NT):
                finish(t)

        @block.gpsimd
        def _(pool):
            tt = nc.gpsimd.tensor_tensor
            r = slice(0, TT)
            nc.gpsimd.memset(expo[:, :], -0.5).then_inc(s_p, 1)
            for g in range(G):
                nc.gpsimd.memset(aT1[:, :, g * GN + GB * S:(g + 1) * GN], 0.0)
            pool.wait_ge(d_const, 16)
            nc.gpsimd.tensor_copy(identb[:, :], ident[:, :])
            nc.gpsimd.tensor_copy(causal_sb[:, :], causal_f[:, :])
            nc.gpsimd.tensor_copy(rowsel_sb[:, :], rowsel_f[:, :])
            pool.wait_ge(s_p, 1)

            def power(k, t):
                pool.wait_ge(var_ready[k], t + 1)
                tt(rstd[r, k, t, :], vare[r, k, t, :], expo[r, 0:1], ALU.pow).then_inc(rstd_ready[k], 1)

            q = qk_c[r, 0:E].rearrange("p (n a d) -> p n a d", n=H0, a=2)
            k_ = qk_c[r, E:2 * E].rearrange("p (n a d) -> p n a d", n=H0, a=2)

            def products(t):
                pool.wait_ge(rope_ready, t + 1)
                tt(prod[r, 1], q[:, :, 1, :].unsqueeze(2).to_broadcast([TT, H0, H0, D0]),
                   k_[:, :, 1, :].unsqueeze(1).to_broadcast([TT, H0, H0, D0]), ALU.mult).then_inc(prod1_ready, 1)

            def value_products(t):
                pool.wait_ge(amix_ready, t + 1)
                nv = H0 - NV
                tt(prodv[r, NV:H0], amix[r, NV:H0].unsqueeze(2).to_broadcast([TT, nv, 2 * D0, H0]),
                   v0[r, t % 2, :].rearrange("p (m e) -> p e m", m=H0).unsqueeze(1).to_broadcast([TT, nv, 2 * D0, H0]),
                   ALU.mult).then_inc(prodv_ready, 1)

            def rotary(t):
                pool.wait_ge(qkv_copied, 2 * t + 1)
                if t == 0:
                    pool.wait_ge(d_rope, 16)
                else:
                    pool.wait_ge(rope_ready, t)
                half = D0 // 2
                x = qk[r, :].rearrange("p (g a d) -> p g a d", a=2, d=half)
                xs = qk_s[r, :].rearrange("p (g a d) -> p g a d", a=2, d=half)
                for a in range(2):
                    sin = rope_sb[r, t, 1, a * half:(a + 1) * half].unsqueeze(1).to_broadcast([TT, 4 * H0, half])
                    last = tt(xs[:, :, a, :], x[:, :, 1 - a, :], sin, ALU.mult)
                last.then_inc(rope_s_ready, 1)

            def rms_power(t):
                pool.wait_ge(ms_ready, t + 1)
                tt(ms[r, t % 2, 1, :], ms[r, t % 2, 0, :], expo[r, 0:H0], ALU.pow).then_inc(rms_ready, 1)

            def repeat(p):
                if p % (PAIRS // G) == 0:
                    pool.wait_ge(copied[3], GT * (2 * p // PAIRS + 1))
                if p >= 2:
                    pool.wait_ge(v1_done, p - 1)
                for i in range(2):
                    for c in range(EC):
                        last = nc.gpsimd.tensor_copy(
                            x3[:, p % 2, i, c],
                            x1T[:, c, pair_cols(p, i)].unsqueeze(1).to_broadcast([P, KT, S]))
                last.then_inc(x3_ready, 1)

            def route(t, step_):
                if step_ == 0:
                    power(3, t)
                elif step_ == 1:
                    pool.wait_ge(copied[4], t + 1)
                    if t >= 2:
                        pool.wait_ge(xm_ready, t - 1)
                    nc.gpsimd.tensor_copy(x3_hi[:, t % 2], x3T[:, :, tile_cols(t)]).then_inc(s_p, 1)
                    pool.wait_ge(s_p, t + 2)
                    tt(x3_lo[:, t % 2], x3T[:, :, tile_cols(t)], x3_hi[:, t % 2].bitcast(F32),
                       ALU.subtract).then_inc(x3_split, 1)

            for t in range(-1, NT + 2):
                if 0 <= t < NT:
                    products(t)
                if 1 <= t <= NT:
                    rms_power(t - 1)
                if t == NT - 1:
                    repeat(0)
                if t < 1:
                    power(0, t + 1)
                if 1 <= t < NT - 1:
                    rotary(t + 1)
                if 1 <= t < NT - 2:
                    power(0, t + 2)
                if t >= 2:
                    power(2, t - 2)
                if 0 <= t < NT:
                    value_products(t)
                if t == NT - 1:
                    repeat(1)
                if t < 1:
                    rotary(t + 1)
                if t == 0:
                    power(0, 2)
                if 1 <= t <= NT:
                    power(1, t - 1)
                if t == -1:
                    pool.wait_ge(d_w0, 16)
                    tt(wf_sb[:], wf_sb[:], disha_sb.unsqueeze(1).to_broadcast([P, EC, E]), ALU.add).then_inc(s_setup, 1)

            for p in range(PAIRS):
                if p + 2 < PAIRS:
                    repeat(p + 2)
                for half in range(2):
                    for t, step_ in routes(slot_of(p, half)):
                        route(t, step_)

            pool.wait_ge(d_tail, 16)

            def residual(t):
                pool.wait_ge(xn_ready[3], t + 1)
                if t >= 2:
                    pool.wait_ge(yo_ready, t - 1)
                tt(xbo[r, t % 2, :], xn[r, t, :], bo_sb[r, :], ALU.add).then_inc(xbo_ready, 1)
                tt(hb[r, t % 2, :], h[r, t, :], beta_sb[r, :], ALU.add).then_inc(hb_ready, 1)

            def experts_low(n):
                pool.wait_ge(ff_ready, n + 1)
                g, f = n // FC, n % FC
                tt(hT_lo[:, f, g * GN:(g + 1) * GN], hT[:, n % 2, :],
                   hT_hi[:, f, g * GN:(g + 1) * GN].bitcast(F32), ALU.subtract).then_inc(ff_split, 1)
                if n >= 2 and 2 * (n - 2) < FC:
                    pool.wait_ge(wo2_hi_ready, n - 1)
                    two = slice(2 * (n - 2), 2 * (n - 1))
                    tt(wo2_lo[:, two, :], wo2_sb[:, two, :], wo2_hi[:, two, :].bitcast(F32),
                       ALU.subtract).then_inc(wo2_lo_ready, 1)

            def norm_scale(t):
                power(4, t)
                if t + 2 < NT:
                    residual(t + 2)

            for t, step_ in routes(slot_of(PAIRS, 0)):
                route(t, step_)
            experts_low(0)
            for f in range(EARLY_CHUNKS, FC):
                for t, step_ in routes(slot_of(PAIRS, 0) + f - EARLY_CHUNKS + 1):
                    route(t, step_)
                experts_low(f - 1)
            residual(0)
            residual(1)
            for f in range(FC):
                experts_low(FC + f - 1)
                if f % 2 == 0 and 2 <= f and f // 2 - 1 < GT:
                    norm_scale(f // 2 - 1)
            experts_low(G * FC - 1)
            for t in range(GT, NT):
                norm_scale(t)


def rope_tables():
    inv = (1.0 / np.float32(10000.0) ** (np.arange(0, D0, 2, dtype=np.float32) / np.float32(D0))).astype(np.float32)
    slot = np.arange(N) % GN
    pos = (slot % S).astype(np.float32)
    f = pos[:, None] * inv[None, :]
    cos, sin = np.cos(f), np.sin(f)
    t = np.stack([np.concatenate([cos, cos], 1), np.concatenate([-sin, sin], 1)], 1).astype(np.float32)
    return np.ascontiguousarray(t.reshape(NT, TT, 2, D0).transpose(1, 0, 2, 3))


def kernel(x, cls_tok, L0_tok_W, L0_tok_b, L0_tok_cls_token, L0_tok_pos_embed, L0_attn_Wq, L0_attn_Wk,
           L0_attn_Wv, L0_attn_Wo, L0_attn_lambda_q1, L0_attn_lambda_k1, L0_attn_lambda_q2,
           L0_attn_lambda_k2, L0_attn_ln_w, L0_attn_ln_b, L0_ffn_weight, L0_ffn_disha, L1_attn_q_proj,
           L1_attn_k_proj, L1_attn_v_proj, L1_attn_o_proj, L1_ffn_W_router, L1_ffn_W1, L1_ffn_b1,
           L1_ffn_Wo, L1_ffn_bo, L1_ffn_ln_gamma, L1_ffn_ln_beta):
    from concourse import bacc
    from concourse.bass_utils import run_bass_kernel_spmd

    a = np.asarray

    def chunks(w):
        w = a(w)
        return np.ascontiguousarray(w.reshape(w.shape[0] // P, P, w.shape[1]).transpose(1, 0, 2))

    def tiled(v, reps):
        return np.concatenate([a(v)] * reps, axis=0)

    pt = a(x).reshape(B, CIN, NP, PATCH, NP, PATCH).transpose(0, 2, 4, 1, 3, 5).reshape(B, NP * NP, PD)
    slots = np.zeros((G, GN, PD), np.float32)
    for b in range(B):
        at = (b % GB) * S
        slots[b // GB, at + 2:at + S] = pt[b]
    patches = np.ascontiguousarray(slots.reshape(NT, TT, PC, P).transpose(3, 0, 2, 1))
    sel = np.zeros((ROWS, N), np.float32)
    for g in range(G):
        for n in range(GB * S):
            s = n % S
            for row in ([0], [1, 3], [2, 3 + s - 1])[min(s, 2)]:
                sel[row, g * GN + n] = 1.0
    rows = np.concatenate([a(cls_tok).reshape(1, E), a(L0_tok_cls_token).reshape(1, E),
                           a(L0_tok_b).reshape(1, E), a(L0_tok_pos_embed).reshape(S - 1, E)], 0)
    order = np.arange(E).reshape(2 * H0, D0 // 2, 2).transpose(0, 2, 1).reshape(E)
    wqkv = chunks(np.concatenate([a(L0_attn_Wq)[:, order], a(L0_attn_Wk)[:, order], a(L0_attn_Wv)], 1))
    lam = np.stack([a(L0_attn_lambda_q1), a(L0_attn_lambda_k1), a(L0_attn_lambda_q2), a(L0_attn_lambda_k2)])
    lam = np.ascontiguousarray(np.broadcast_to(lam.reshape(1, 2, 2, D0), (P, 2, 2, D0)))
    lnwb = np.stack([tiled(L0_attn_ln_w, P // (2 * D0)), tiled(L0_attn_ln_b, P // (2 * D0))], 1)
    part = np.arange(P)
    hmask = (part[:, None] // D1 == np.arange(HC)[None, :]).astype(np.float32)
    vmask = np.zeros((KR, KT, D1), np.float32)
    vones = np.zeros((KR, 2, KC, 2, KT, VW), np.float32)
    for j in range(KT):
        vmask[j * S:(j + 1) * S, j] = 1.0
        vones[j * S:(j + 1) * S, :, :, :, j, D1] = 1.0
    causal = np.where(np.tril(np.ones((S, S), bool)), 0.0, MASKED).astype(np.float32)
    rowsel = (part[None, :] % HALF == np.arange(S)[:, None]).astype(np.float32)
    w1 = np.ascontiguousarray(a(L1_ffn_W1).reshape(NX, EC, P, FF).transpose(2, 1, 0, 3))
    low = np.array([[0.0, 1.0]] * NX + [[1.0, -1.0]] * NX, np.float32)
    tie = np.arange(NX, 0, -1).astype(np.float32)
    tail = np.concatenate([a(L1_ffn_bo), a(L1_ffn_ln_gamma), a(L1_ffn_ln_beta), tie])
    tail = np.ascontiguousarray(np.broadcast_to(tail[None, :], (P, tail.size)))

    small = {"lam": lam, "lnwb": lnwb, "hmask": hmask, "vmask": vmask, "causal": causal, "rowsel": rowsel,
             "ident": np.eye(P, dtype=np.float32)}
    const, at = np.zeros((P, sum(CONSTS.values())), np.float32), 0
    for name, width in CONSTS.items():
        v = small[name].reshape(small[name].shape[0], width)
        const[0:v.shape[0], at:at + width] = v
        at += width
    w0 = np.concatenate([chunks(L0_attn_Wo), chunks(a(L0_ffn_weight).T), tiled(L0_ffn_disha, 2)[:, None, :]], 1)

    arrays = {
        "patches": patches, "tok_w": chunks(a(L0_tok_W).T), "rows_sel": np.concatenate([rows, sel], 1),
        "const": const, "wqkv": wqkv, "rope": rope_tables(), "w0": w0, "wq1": chunks(a(L1_attn_q_proj).T),
        "wk1": chunks(a(L1_attn_k_proj).T), "wv1": chunks(a(L1_attn_v_proj).T),
        "wo1": chunks(a(L1_attn_o_proj).T), "vones": vones, "wr": chunks(L1_ffn_W_router),
        "w1": w1, "b1": tiled(L1_ffn_b1, 2), "low": low, "wo2": chunks(L1_ffn_Wo), "tail": tail,
    }
    nc = bacc.Bacc("TRN2", target_bir_lowering=False, num_devices=1)
    named, args = {}, []
    for name, v in arrays.items():
        v = np.ascontiguousarray(v)
        named[f"in_{name}"] = v
        args.append(nc.dram_tensor(f"in_{name}", v.shape, mybir.dt.from_np(v.dtype), kind="ExternalInput").ap())
    args.append(nc.dram_tensor("out_0", (N, E), F32, kind="ExternalOutput").ap())
    tower_kernel(nc, *args)
    res = run_bass_kernel_spmd(nc, [named], core_ids=[0])
    got = a(res.results[0]["out_0"]).reshape(G, GN, E)[:, 0:GB * S].reshape(B, S, E)
    return np.ascontiguousarray(got)
```
